# Optimizing a Trainium2 kernel written in Bass

```python
import numpy as np
import jax
import jax.numpy as jnp

def _softmax(x, axis=-1):
    return jax.nn.softmax(x, axis=axis)

def _gelu(x):
    return jax.nn.gelu(x, approximate=True)

def _silu(x):
    return jax.nn.silu(x)

def _sigmoid(x):
    return jax.nn.sigmoid(x)

def _layernorm(x, axis=-1, eps=1e-05):
    m = jnp.mean(x, axis=axis, keepdims=True)
    v = jnp.var(x, axis=axis, keepdims=True)
    return (x - m) / jnp.sqrt(v + eps)

def _scatter_add(tgt, idx, src, axis=0):
    return tgt.at[idx].add(src)

def _segment_sum(src, seg, n):
    return jax.ops.segment_sum(src, seg, n)
kernel_name = 'mk_adj_resnorm_d2_adj_r2_f76ee5'

def setup_inputs(seed: int=0):
    np.random.seed(seed)
    _w = jnp.asarray

    def _rec_inputs():
        import jax
        import jax.numpy as jnp
        _gk = jax.random.key(seed)
        x = 7.22e-05 + 1 * jax.random.normal(jax.random.fold_in(_gk, 1), (16, 512, 128), jnp.float32)
        _w = (1.0 + jnp.arange(512, dtype=jnp.float32)) ** (-0.5)
        _w = _w / _w.mean()
        _pij = jnp.clip(0.015625 * _w[:, None] * _w[None, :], 0.0, 1.0)
        _a = jax.random.uniform(jax.random.fold_in(_gk, 2), (16, 512, 512)) < _pij
        _af = _a.astype(jnp.float32)
        adj = _af
        _nm = jnp.ones((16, 512), dtype=bool)
        nodemask = jnp.where(_nm, 1.0, 0.0).astype(jnp.float32)
        return (x, adj, nodemask)
    x, adj, nodemask = _rec_inputs()

    def _L0_gnn_setup():
        import jax, jax.numpy as jnp
        import numpy as np
        B, N, D, C, L = (64, 256, 128, 128, 5)
        EDGE_P = 0.02

        def _gru_cell(m, h, w_ih, w_hh, b_ih, b_hh):
            gi = m @ w_ih.T + b_ih
            gh = h @ w_hh.T + b_hh
            i_r, i_z, i_n = jnp.split(gi, 3, axis=-1)
            h_r, h_z, h_n = jnp.split(gh, 3, axis=-1)
            r = jax.nn.sigmoid(i_r + h_r)
            z = jax.nn.sigmoid(i_z + h_z)
            n = jnp.tanh(i_n + r * h_n)
            return (1.0 - z) * n + z * h
        key = jax.random.key(seed)
        ks = jax.random.split(key, 8)
        x = jax.random.normal(ks[0], (B, N, D), dtype=jnp.float32)
        adj = (jax.random.uniform(ks[1], (B, N, N)) < EDGE_P).astype(jnp.float32)
        mask = jnp.ones((B, N), dtype=jnp.float32)
        s = 1.0 / np.sqrt(C).astype(np.float32)
        weight = jax.random.uniform(ks[2], (L, C, C), minval=-s, maxval=s, dtype=jnp.float32)
        w_ih = jax.random.uniform(ks[3], (3 * C, C), minval=-s, maxval=s, dtype=jnp.float32)
        w_hh = jax.random.uniform(ks[4], (3 * C, C), minval=-s, maxval=s, dtype=jnp.float32)
        b_ih = jax.random.uniform(ks[5], (3 * C,), minval=-s, maxval=s, dtype=jnp.float32)
        b_hh = jax.random.uniform(ks[6], (3 * C,), minval=-s, maxval=s, dtype=jnp.float32)
        return dict(x=x, adj=adj, mask=mask, weight=weight, w_ih=w_ih, w_hh=w_hh, b_ih=b_ih, b_hh=b_hh)
    _L0_gnn_all = _L0_gnn_setup()
    _L0_gnn_in = {k: v for k, v in _L0_gnn_all.items() if k in ('weight', 'w_ih', 'w_hh', 'b_ih', 'b_hh')}
    del _L0_gnn_all

    def _L1_gnn_setup():
        import jax, jax.numpy as jnp
        import numpy as np
        GROUPS = [list(range(25)), [0, 1, 2, 3, 4, 5, 6, 7, 8], [0, 9, 10, 11, 12, 13, 14], [6, 7, 8, 12, 13, 14], [3, 4, 5, 9, 10, 11]]
        B, N, D_IN, D_HID = (4096, 25, 128, 256)

        def _graph_conv(x, adj, W, b):
            n = adj.shape[-1]
            A = adj + jnp.eye(n, dtype=adj.dtype)
            deg = jnp.sum(A, axis=-1)
            deg_safe = jnp.where(deg == 0, 1.0, deg)
            dinv = jnp.where(deg == 0, 0.0, deg_safe ** (-0.5))
            norm_adj = dinv[:, :, None] * A * dinv[:, None, :]
            support = jnp.einsum('bnd,de->bne', x, W)
            out = jnp.einsum('bnm,bme->bne', norm_adj, support) + b
            return jax.nn.relu(out)
        key = jax.random.key(seed)
        ks = jax.random.split(key, 7)
        s1 = float(np.sqrt(6.0 / (D_IN + D_HID)))
        s2 = float(np.sqrt(6.0 / (D_HID + D_IN)))
        return {'x': jax.random.normal(ks[0], (B, N, D_IN), dtype=jnp.float32), 'adj': jax.random.uniform(ks[1], (B, N, N), dtype=jnp.float32), 'W1': jax.random.uniform(ks[2], (5, D_IN, D_HID), jnp.float32, -s1, s1), 'b1': jnp.zeros((5, D_HID), dtype=jnp.float32), 'W2': jax.random.uniform(ks[3], (5, D_HID, D_IN), jnp.float32, -s2, s2), 'b2': jnp.zeros((5, D_IN), dtype=jnp.float32), 'fusion_w': jnp.ones((5,), dtype=jnp.float32)}
    _L1_gnn_all = _L1_gnn_setup()
    _L1_gnn_in = {k: v for k, v in _L1_gnn_all.items() if k in ('W1', 'b1', 'W2', 'b2', 'fusion_w')}
    del _L1_gnn_all
    return {'x': x, 'adj': adj, 'nodemask': nodemask, 'L0_gnn_weight': _L0_gnn_in['weight'], 'L0_gnn_w_ih': _L0_gnn_in['w_ih'], 'L0_gnn_w_hh': _L0_gnn_in['w_hh'], 'L0_gnn_b_ih': _L0_gnn_in['b_ih'], 'L0_gnn_b_hh': _L0_gnn_in['b_hh'], 'L1_gnn_W1': _L1_gnn_in['W1'], 'L1_gnn_b1': _L1_gnn_in['b1'], 'L1_gnn_W2': _L1_gnn_in['W2'], 'L1_gnn_b2': _L1_gnn_in['b2'], 'L1_gnn_fusion_w': _L1_gnn_in['fusion_w']}

def reference(x, adj, nodemask, L0_gnn_weight, L0_gnn_w_ih, L0_gnn_w_hh, L0_gnn_b_ih, L0_gnn_b_hh, L1_gnn_W1, L1_gnn_b1, L1_gnn_W2, L1_gnn_b2, L1_gnn_fusion_w):
    import jax
    import jax.numpy as jnp

    def _L0_gnn_ref(x, adj, mask, weight, w_ih, w_hh, b_ih, b_hh):
        import jax, jax.numpy as jnp
        import numpy as np
        B, N, D, C, L = (64, 256, 128, 128, 5)
        EDGE_P = 0.02

        def _gru_cell(m, h, w_ih, w_hh, b_ih, b_hh):
            gi = m @ w_ih.T + b_ih
            gh = h @ w_hh.T + b_hh
            i_r, i_z, i_n = jnp.split(gi, 3, axis=-1)
            h_r, h_z, h_n = jnp.split(gh, 3, axis=-1)
            r = jax.nn.sigmoid(i_r + h_r)
            z = jax.nn.sigmoid(i_z + h_z)
            n = jnp.tanh(i_n + r * h_n)
            return (1.0 - z) * n + z * h
        A = (adj != 0).astype(x.dtype)
        h = x
        for l in range(weight.shape[0]):
            m = jnp.einsum('bnd,de->bne', h, weight[l])
            agg = jnp.einsum('bij,bid->bjd', A, m)
            h = _gru_cell(agg, h, w_ih, w_hh, b_ih, b_hh)
        return h * mask[..., None]

    def _L1_gnn_ref(x, adj, W1, b1, W2, b2, fusion_w):
        import jax, jax.numpy as jnp
        import numpy as np
        GROUPS = [list(range(25)), [0, 1, 2, 3, 4, 5, 6, 7, 8], [0, 9, 10, 11, 12, 13, 14], [6, 7, 8, 12, 13, 14], [3, 4, 5, 9, 10, 11]]
        B, N, D_IN, D_HID = (4096, 25, 128, 256)

        def _graph_conv(x, adj, W, b):
            n = adj.shape[-1]
            A = adj + jnp.eye(n, dtype=adj.dtype)
            deg = jnp.sum(A, axis=-1)
            deg_safe = jnp.where(deg == 0, 1.0, deg)
            dinv = jnp.where(deg == 0, 0.0, deg_safe ** (-0.5))
            norm_adj = dinv[:, :, None] * A * dinv[:, None, :]
            support = jnp.einsum('bnd,de->bne', x, W)
            out = jnp.einsum('bnm,bme->bne', norm_adj, support) + b
            return jax.nn.relu(out)
        norm_w = jax.nn.softmax(fusion_w)
        fused = jnp.zeros_like(x)
        for g, idx_list in enumerate(GROUPS):
            idx = jnp.asarray(idx_list)
            x_g = x[:, idx, :]
            adj_g = adj[:, idx][:, :, idx]
            h = _graph_conv(x_g, adj_g, W1[g], b1[g])
            out_g = _graph_conv(h, adj_g, W2[g], b2[g])
            fused = fused.at[:, idx, :].add(norm_w[g] * out_g)
        return fused
    x = _layernorm(x + _L0_gnn_ref(x, adj, nodemask, L0_gnn_weight, L0_gnn_w_ih, L0_gnn_w_hh, L0_gnn_b_ih, L0_gnn_b_hh), axis=-1)
    x = _layernorm(x + _L1_gnn_ref(x, adj, L1_gnn_W1, L1_gnn_b1, L1_gnn_W2, L1_gnn_b2, L1_gnn_fusion_w), axis=-1)
    return x

_drawn_inputs = setup_inputs


def setup_inputs(seed=0):
    import zlib

    import numpy as np

    out = dict(_drawn_inputs(seed))
    spreads = {'L1_gnn_b1': (0.0, 0.8), 'L1_gnn_b2': (0.0, 2.0), 'L1_gnn_fusion_w': (1.0, 0.6)}
    factors = {'L1_gnn_W1': 3.957, 'L1_gnn_W2': 3.175}
    for name, (base, spread) in spreads.items():
        noise = np.random.default_rng([zlib.crc32(name.encode()), seed]).standard_normal(out[name].shape)
        drawn = base * np.exp(spread * noise) if base else spread * noise
        out[name] = jnp.asarray(drawn.astype(out[name].dtype))
    for name, factor in factors.items():
        out[name] = (out[name] * factor).astype(out[name].dtype)
    return out
```

```python
from contextlib import ExitStack

import concourse.bass as bass
from concourse import mybir

ALU = mybir.AluOpType
ACT = mybir.ActivationFunctionType
AX_X = mybir.AxisListType.X
F32 = mybir.dt.float32
F16 = mybir.dt.float16
U32 = mybir.dt.uint32

P = 128
B, N, D = 16, 512, 128
L = 5
NI = N // P
K = B * L
LAST = K - B
GROUPS = [list(range(25)), [0, 1, 2, 3, 4, 5, 6, 7, 8], [0, 9, 10, 11, 12, 13, 14],
          [6, 7, 8, 12, 13, 14], [3, 4, 5, 9, 10, 11]]
G = len(GROUPS)
HID = 256
NH = HID // P
Q = 4
S = P // Q
NC = B // Q
EPS = 1e-5
WSCALE = 1024.0
UNSCALE = 1.0 / WSCALE

MIDDLE = (14, 62)
SEGMENTS = [0, (1, 13), 13, MIDDLE, 62, 63, 64, 65, 66, 67, 68, (69, 77), 77, 78, 79]
TAIL = [80, 81, 82, 83, 84]


def walk(eng, iteration, before=None):
    for seg in SEGMENTS:
        if isinstance(seg, int):
            if before and seg in before:
                before[seg]()
            iteration(seg, seg)
        else:
            with eng.Fori(seg[0], seg[1] - 3, 4) as k0:
                for j in range(4):
                    iteration(k0 + j, seg[0] + j)
    for k in TAIL:
        iteration(k, k)


def graph_of(k):
    return k % B if isinstance(k, int) else (k & (B - 1))


def layer_of(k):
    return k // B if isinstance(k, int) else (k >> 4)


def half(k):
    return k // 2 if isinstance(k, int) else (k >> 1)


def quarter(k):
    return k // 4 if isinstance(k, int) else (k >> 2)


def runs_of(members):
    runs = []
    for m in members:
        if runs and runs[-1][-1] == m - 1:
            runs[-1].append(m)
        else:
            runs.append([m])
    return runs


def one(i):
    return slice(i, i + 1) if isinstance(i, int) else bass.ds(i, 1)


def graph_net_kernel(nc, x, adj, nodemask, weight, w_ih, w_hh, b_ih, b_hh, W1, b1, W2, b2, fusion_w, out):
    ctx = ExitStack()
    with ctx:
        def sb(name, shape, dt):
            return ctx.enter_context(nc.sbuf_tensor(name, shape, dt))

        def pb(name, shape):
            return ctx.enter_context(nc.psum_tensor(name, shape, F32))

        def sem(name):
            return ctx.enter_context(nc.semaphore(name))

        A16 = sb("A16", [P, B, NI, N], F16)
        HT = sb("HT", [P, B, 2, N], F16)
        H = sb("H", [P, B, N], F32)
        AS = sb("AS", [P, 2, NI, N], F32)
        XS = sb("XS", [P, 4, NI, D], F32)
        NAT = sb("NAT", [P, 2, 2, NI, D], F16)
        AG = sb("AG", [P, 2, 2, N], F16)
        HF = sb("HF", [P, 2, N], F32)
        Y = sb("Y", [P, 4, NI, D], F32)
        R = sb("R", [P, N], F32)
        Z = sb("Z", [P, N], F32)
        T = sb("T", [P, N], F32)
        NN = sb("NN", [P, N], F32)
        E = sb("E", [P, N], F32)
        WC = sb("WC", [P, L, 2, 3, D], F16)
        WH = sb("WH", [P, 2, 3, D], F16)
        BRZ = sb("BRZ", [P, 2], F32)
        BHN = sb("BHN", [P, 1], F32)
        IDF = sb("IDF", [P, P], F32)
        ID16 = sb("ID16", [P, P], F16)
        I32 = sb("I32", [P, S], F32)
        rows_m, rows_i, rows_h, rows_1 = 0, B * NI, B * NI + 3, B * NI + 6
        ROWS = sb("ROWS", [rows_1 + G * NH, P], F32)
        COLS = sb("COLS", [P, rows_1 + G * NH], F32)
        MASK = COLS[:, 0:rows_i].rearrange("p (b i) -> p b i", b=B)
        BI = COLS[:, rows_i:rows_h]
        BH = COLS[:, rows_h:rows_1]
        B1 = COLS[:, rows_1:].rearrange("p (g j) -> p g j", g=G)
        ST = sb("ST", [P, NI, 6], F32)
        MV = sb("MV", [P, 4, NI, 2], F32)
        VE = sb("VE", [P, 4, NI + 1], F32)
        RS = sb("RS", [P, 4, NI + 1], F32)
        NB = sb("NB", [P, 4, NI], F32)
        NHALF = sb("NHALF", [P, G * NC], F32)
        BD = sb("BD", [P, G, NC, Q, S], F32)
        X1 = sb("X1", [P, NC, D], F32)
        CM = sb("CM", [P, G, S], F32)
        CMT = sb("CMT", [P, G, S], F32)
        FW = sb("FW", [P, G], F32)
        FS = sb("FS", [P, 4], F32)
        MS = sb("MS", [P, G], F32)
        DEG = sb("DEG", [P, 3, G * NC], F32)
        DG = [DEG[:, i, :] for i in range(3)]

        scr = A16[:, B - 4:B, :, :].rearrange("p b i n -> p (b i n)").bitcast(F32)
        off = [0]

        def scratch(n):
            off[0] += n
            assert off[0] <= 4 * NI * N // 2
            return scr[:, off[0] - n:off[0]]

        WL = scratch(L * D).rearrange("p (l e) -> p l e", l=L)
        WLT = scratch(L * D).rearrange("p (l e) -> p l e", l=L)
        WI = scratch(3 * D).rearrange("p (g e) -> p g e", g=3)
        WHS = scratch(3 * D).rearrange("p (g e) -> p g e", g=3)
        WIT = scratch(3 * D)
        y_flat = Y[:, :, :, :].rearrange("p s i d -> p (s i d)")
        y_end = G * NC * S
        AM = y_flat[:, 0:y_end].rearrange("p (g c m) -> p g c m", g=G, c=NC)
        AT = y_flat[:, y_end:2 * y_end].rearrange("p (g c m) -> p g c m", g=G, c=NC)
        AB = y_flat[:, 2 * y_end:2 * y_end + NC * S].rearrange("p (c m) -> p c m", c=NC)
        AMF = y_flat[:, 0:y_end].rearrange("p (x m) -> p x m", m=S)

        as_flat = AS[:, :, :, :].rearrange("p s i n -> p (s i n)")
        W1S = as_flat[:, 0:G * HID].rearrange("p (g e) -> p g e", g=G)
        W2S = as_flat[:, G * HID:2 * G * HID].rearrange("p (g j e) -> p g j e", g=G, j=NH)
        B2S = as_flat[:, 2 * G * HID:2 * G * HID + G * D].rearrange("p (g e) -> p g e", g=G)
        w_end = 2 * G * HID + G * D
        YM = as_flat[:, w_end:w_end + NI * D].rearrange("p (i d) -> p i d", i=NI)
        lateA = A16[:, :, :, :].rearrange("p b i n -> p (b i n)").bitcast(F32)
        YT = lateA[:, 0:G * N].rearrange("p (g n) -> p g n", g=G)
        H1 = lateA[:, G * N:3 * G * N].rearrange("p (g j n) -> p g j n", g=G, j=NH)
        S2 = lateA[:, 3 * G * N:4 * G * N].rearrange("p (g c e) -> p g c e", g=G, c=NC)
        U = lateA[:, 4 * G * N:(4 * G + 2) * N].rearrange("p (s c e) -> p s c e", s=2, c=NC)
        FU = lateA[:, (4 * G + 2) * N:(4 * G + 3) * N].rearrange("p (c e) -> p c e", c=NC)
        ZO = lateA[:, (4 * G + 3) * N:(4 * G + 4) * N].rearrange("p (c e) -> p c e", c=NC)

        pAG = pb("pAG", [P, N])
        pR = pb("pR", [P, N])
        pZ = pb("pZ", [P, N])
        pIN = pb("pIN", [P, N])
        pHN = pb("pHN", [P, N])
        pF = pb("pF", [P, N])
        pT = pb("pT", [P, 2, N])

        ld_x = [sem(f"ld_x{i}") for i in range(4)]
        ld_a = [sem(f"ld_a{i}") for i in range(2)]
        ld_w = sem("ld_w")
        ld_c = sem("ld_c")
        ld_f = sem("ld_f")
        ld_g = sem("ld_g")
        st_y = [sem(f"st_y{i}") for i in range(4)]
        st_z = sem("st_z")
        ident = sem("ident")
        masks0 = sem("masks0")
        prep_t = sem("prep_t")
        prep_v = sem("prep_v")
        prep_a = sem("prep_a")
        wsplit_l = sem("wsplit_l")
        fw_max = sem("fw_max")
        chain = sem("chain")
        deg_v = sem("deg_v")
        BD_STEPS = 4 + Q
        bd_p = sem("bd_p")
        am_p = sem("am_p")
        nat_hi = sem("nat_hi")
        nat_lo = sem("nat_lo")
        a_cast = sem("a_cast")
        t_mm = sem("t_mm")
        t_ev = sem("t_ev")
        hm = sem("hm")
        ag_mm = sem("ag_mm")
        ag_hi = sem("ag_hi")
        ag_lo = sem("ag_lo")
        r_mm = sem("r_mm")
        in_mm = sem("in_mm")
        z_mm = sem("z_mm")
        sig_r = sem("sig_r")
        sig_z = sem("sig_z")
        t_v = sem("t_v")
        u_v = sem("u_v")
        n_a = sem("n_a")
        d_v = sem("d_v")
        e_v = sem("e_v")
        h_v = sem("h_v")
        h_hi = sem("h_hi")
        h_lo = sem("h_lo")
        f_mm = sem("f_mm")
        f_ym = sem("f_ym")
        f_y = sem("f_y")
        f_st = sem("f_st")
        f_mv = sem("f_mv")
        f_var = sem("f_var")
        f_rs = sem("f_rs")
        f_nb = sem("f_nb")
        f_on = sem("f_on")
        c_a = sem("c_a")
        c_ae = sem("c_ae")
        c_b = sem("c_b")
        c_be = sem("c_be")
        c_s = sem("c_s")
        c_se = sem("c_se")
        c_d = sem("c_d")
        c_u = sem("c_u")
        c_m = sem("c_m")
        c_f = sem("c_f")
        z_v = sem("z_v")
        z_p = sem("z_p")
        z_o = sem("z_o")

        block = ctx.enter_context(nc.Block())

        @block.sync
        def _(sp):
            def load_x(slot, b):
                sp.dma_start(XS[:, slot, :, :],
                             x[one(b), :, :].rearrange("b (i p) d -> p (b i) d", p=P)).then_inc(ld_x[slot], 16)

            def load_a(slot, b):
                sp.dma_start(AS[:, slot, :, :],
                             adj[one(b), :, :].rearrange("b (i p) n -> p (b i) n", p=P)).then_inc(ld_a[slot], 16)

            load_x(0, 0)
            for row, src in ((rows_m, nodemask.rearrange("b (i p) -> (b i) p", p=P)),
                             (rows_i, b_ih.rearrange("(g p) -> g p", p=P)),
                             (rows_h, b_hh.rearrange("(g p) -> g p", p=P)),
                             (rows_1, b1.rearrange("g (j p) -> (g j) p", p=P))):
                sp.dma_start(ROWS[row:row + src.shape[0], :], src).then_inc(ld_w, 16)
            sp.dma_start(WI, w_ih.rearrange("(g c) d -> c g d", c=P)).then_inc(ld_w, 16)
            sp.dma_start(WHS, w_hh.rearrange("(g c) d -> c g d", c=P)).then_inc(ld_w, 16)
            sp.dma_start(WL, weight.rearrange("l d e -> d l e")).then_inc(ld_w, 16)
            load_a(0, 0)
            sp.dma_start(FW[:, :], fusion_w.partition_broadcast(P)).then_inc(ld_f, 16)
            load_x(1, 1)
            load_x(2, 2)
            load_x(3, 3)
            load_a(1, 1)
            with sp.Fori(2, 11, 4) as b0:
                for j in range(4):
                    sp.wait_ge(a_cast, b0 + j - 1)
                    load_a(j % 2, b0 + j)
                    sp.wait_ge(nat_lo, b0 + j - 1)
                    load_x(j, b0 + j + 2)
            for b in range(14, B):
                sp.wait_ge(a_cast, b - 1)
                load_a(b % 2, b)
            for b in range(4):
                sp.wait_ge(nat_lo, B - 3 + b)
                load_x(b, b)
            sp.wait_ge(a_cast, B)
            sp.dma_start(W1S, W1.rearrange("g d e -> d g e")).then_inc(ld_g, 16)
            sp.dma_start(W2S, W2.rearrange("g (j h) e -> h g j e", j=NH)).then_inc(ld_g, 16)
            sp.dma_start(B2S, b2.partition_broadcast(P)).then_inc(ld_g, 16)

            def store_y(b, slot):
                sp.wait_ge(f_on, b + 1)
                sp.dma_start(out[one(b), S:P, :].rearrange("b p d -> p (b d)"),
                             Y[S:P, slot, 0, :]).then_inc(st_y[slot], 16)
                sp.dma_start(out[one(b), P:N, :].rearrange("b (i p) d -> p (b i) d", p=P),
                             Y[:, slot, 1:NI, :]).then_inc(st_y[slot], 16)

            with sp.Fori(0, B - 7, 4) as f0:
                for j in range(4):
                    store_y(f0 + j, j)
                    sp.wait_ge(st_y[j], 32 * (quarter(f0 + j) + 1))
                    load_x(j, f0 + j + 4)
            for f in range(B - 4, B):
                store_y(f, f % 4)
            for q in range(Q):
                sp.wait_ge(z_o, 1)
                sp.dma_start(out.rearrange("(c q) n d -> q n c d", q=Q)[q, 0:S],
                             ZO[S * q:S * q + S, :, :]).then_inc(st_z, 16)
            for slot in range(4):
                sp.wait_ge(st_y[slot], 32 * (B // 4))
            sp.wait_ge(st_z, 16 * Q)

        @block.gpsimd
        def _(pool):
            nc.gpsimd.memset(IDF[:, :], 0.0).then_inc(ident, 1)
            pool.wait_ge(ident, 1)
            nc.gpsimd.affine_select(out=IDF[:, :], in_=IDF[:, :], compare_op=ALU.not_equal, fill=1.0,
                                    base=0, pattern=[[-1, P]], channel_multiplier=1).then_inc(ident, 1)
            pool.wait_ge(ident, 2)
            nc.gpsimd.tensor_copy(ID16[:, :], IDF[:, :]).then_inc(ident, 1)
            nc.gpsimd.memset(NHALF[:, :], -0.5)
            nc.gpsimd.memset(CM[:, :, :], 0.0).then_inc(masks0, 1)
            pool.wait_ge(masks0, 1)
            for g, members in enumerate(GROUPS):
                for run in runs_of(members):
                    last = nc.gpsimd.memset(CM[:, g, run[0]:run[-1] + 1], 1.0)
            last.then_inc(masks0, 1)
            for q in range(Q):
                pool.dma_start(AB[S * q:S * q + S, :, :],
                               adj.rearrange("(c q) n m -> q n c m", q=Q)[q, 0:S, :, 0:S]).then_inc(ld_c, 16)
            def natural_lo(k, s):
                pool.wait_ge(nat_hi, k + 1)
                nc.gpsimd.tensor_tensor(NAT[:, s % 2, 1, :, :], XS[:, s % 4, :, :], NAT[:, s % 2, 0, :, :],
                                        ALU.subtract).then_inc(nat_lo, 1)

            def iteration(k, s):
                if LAST <= s - 1 < K:
                    pool.wait_ge(n_a, k)
                    pool.wait_ge(h_v, k - 1)
                    nc.gpsimd.tensor_tensor(E[:, :], H[:, one(graph_of(k - 1)), :], NN[:, :],
                                            ALU.subtract).then_inc(d_v, 1)
                if s + 3 < B:
                    natural_lo(k + 3, s + 3)
                if s + 2 < B:
                    b = graph_of(k + 2)
                    pool.wait_ge(t_ev, k + 3)
                    nc.gpsimd.tensor_tensor(H[:, one(b), :], HT[:, one(b), 0, :], HT[:, one(b), 1, :],
                                            ALU.add).then_inc(hm, 1)
                if LAST <= s - 2 < K:
                    f, slot = k - 2 - LAST, (s - 2) % 4
                    pool.wait_ge(f_ym, f + 1)
                    pool.wait_ge(ld_x[slot], 16 * (B // 4) + 16 * (quarter(f) + 1))
                    nc.gpsimd.tensor_tensor(Y[:, slot, :, :], YM[:, :, :], XS[:, slot, :, :],
                                            ALU.add).then_inc(f_y, 1)
                if LAST <= s - 3 < K:
                    f, w = k - 3 - LAST, (s - 3) % 4
                    pool.wait_ge(f_var, f + 1)
                    nc.gpsimd.tensor_tensor(RS[:, w, :], VE[:, w, :], NHALF[:, 0:NI + 1], ALU.pow).then_inc(f_rs, 1)

            natural_lo(0, 0)
            natural_lo(1, 1)
            natural_lo(2, 2)
            for b in range(2):
                pool.wait_ge(t_ev, b + 1)
                nc.gpsimd.tensor_tensor(H[:, b, :], HT[:, b, 0, :], HT[:, b, 1, :], ALU.add).then_inc(hm, 1)

            def prepare_adjacency():
                g_ = nc.gpsimd
                n = [0]

                def link(ins):
                    n[0] += 1
                    ins.then_inc(bd_p, 1)
                    pool.wait_ge(bd_p, n[0])

                pool.wait_ge(ld_c, 16 * Q)
                for g in range(G):
                    last = g_.tensor_tensor(AM[:, g, :, :], AB[:, :, :],
                                            CM[:, g:g + 1, :].to_broadcast([P, NC, S]), ALU.mult)
                link(last)
                link(g_.tensor_tensor(AMF, AMF, I32[:, None, :].to_broadcast([P, G * NC, S]), ALU.add))
                g_.memset(BD[:, :, :, :, :].rearrange("p g c q s -> p (g c q s)"), 0.0).then_inc(am_p, 1)
                pool.wait_ge(deg_v, 1)
                link(g_.tensor_tensor(DG[1], DG[0], NHALF[:, :], ALU.pow))
                link(g_.tensor_tensor(DG[2], DG[2], DG[1], ALU.mult))
                g_.tensor_tensor(AMF, AMF, DG[2][:, :, None].to_broadcast([P, G * NC, S]), ALU.mult).then_inc(am_p, 1)
                pool.wait_ge(deg_v, 2)
                pool.wait_ge(am_p, 2)
                for q in range(Q):
                    rows = slice(S * q, S * q + S)
                    link(g_.tensor_tensor(BD[rows, :, :, q, :].rearrange("p g c s -> p (g c) s"),
                                            AT[rows, :, :, :].rearrange("p g c m -> p (g c) m"),
                                            DG[2][rows, :, None].to_broadcast([S, G * NC, S]), ALU.mult))

                assert n[0] == BD_STEPS

            walk(pool, iteration, {62: prepare_adjacency})
            pool.wait_ge(z_v, 3)
            nc.gpsimd.tensor_tensor(RS[:, 0, 0:NC], VE[:, 0, 0:NC], NHALF[:, 0:NC], ALU.pow).then_inc(z_p, 1)

        @block.tensor
        def _(pe):
            mm = nc.tensor.matmul
            pe.wait_ge(ident, 2)
            pe.wait_ge(ld_w, 16 * 7)
            for g in range(3):
                nc.tensor.transpose(pR[:, g * D:(g + 1) * D], WI[:, g, :], IDF[:, :])
            last = None
            for g in range(3):
                last = nc.tensor.transpose(pZ[:, g * D:(g + 1) * D], WHS[:, g, :], IDF[:, :])
            last.then_inc(prep_t, 1)
            for l in range(4):
                nc.tensor.transpose(pIN[:, l * D:(l + 1) * D], WL[:, l, :], IDF[:, :])
            nc.tensor.transpose(pHN[:, 0:D], WL[:, 4, :], IDF[:, :]).then_inc(prep_t, 1)
            rows = ROWS.shape[0]
            nc.tensor.transpose(pF[:, 0:rows], ROWS[:, :], IDF[0:rows, 0:rows]).then_inc(prep_t, 1)

            def transpose_step(k, s):
                if s == 0:
                    pe.wait_ge(ident, 3)
                if s < B:
                    pe.wait_ge(nat_lo, k + 1)
                else:
                    pe.wait_ge(h_lo, k - B + 1)
                if s > 0:
                    pe.wait_ge(t_ev, k)
                b = graph_of(k)
                for h in range(2):
                    for i in range(NI):
                        src = (NAT[:, s % 2, h, i, :] if s < B
                               else HT[:, one(b), h, i * P:(i + 1) * P].rearrange("p b n -> p (b n)"))
                        last = mm(pT[:, h, i * P:(i + 1) * P], src, ID16[:, :], start=True, stop=True)
                last.then_inc(t_mm, 1)

            def aggregate(k, s):
                b = graph_of(k)
                if s < B - 1:
                    pe.wait_ge(nat_lo, k + 1)
                    pe.wait_ge(a_cast, k + 1)
                else:
                    if s == B - 1:
                        pe.wait_ge(nat_lo, B)
                        pe.wait_ge(a_cast, B)
                    pe.wait_ge(t_ev, k + 1)
                if s > 0:
                    pe.wait_ge(ag_lo, k)
                for h in range(2):
                    for i in range(NI):
                        last = mm(pAG[:, :], NAT[:, s % 2, h, i, :], A16[:, one(b), i, :],
                                  start=(h == 0 and i == 0), stop=(h == 1 and i == NI - 1))
                last.then_inc(ag_mm, 1)

            def split_product(bank, w_hi, w_lo, v_hi, v_lo, start, stop):
                mm(bank[:, :], w_hi, v_hi, start=start, stop=False)
                mm(bank[:, :], w_hi, v_lo, start=False, stop=False)
                return mm(bank[:, :], w_lo, v_hi, start=False, stop=stop)

            def gates(k, s, between):
                b = graph_of(k)
                l = layer_of(k) if MIDDLE[0] <= s < MIDDLE[1] else s // B
                ht = [HT[:, one(b), h, :] for h in range(2)]
                pe.wait_ge(t_ev, k + 1)
                if s > 0:
                    pe.wait_ge(t_v, k)
                split_product(pHN, WH[:, 0, 2, :], WH[:, 1, 2, :], ht[0], ht[1], True, True)
                if s > 0:
                    pe.wait_ge(sig_r, k)
                split_product(pR, WH[:, 0, 0, :], WH[:, 1, 0, :], ht[0], ht[1], True, False)
                if s > 0:
                    pe.wait_ge(sig_z, k)
                split_product(pZ, WH[:, 0, 1, :], WH[:, 1, 1, :], ht[0], ht[1], True, False)
                between()
                ag = [AG[:, s % 2, h, :] for h in range(2)]

                def wc(h, g):
                    if isinstance(l, int):
                        return WC[:, l, h, g, :]
                    return WC[:, one(l), h, g, :].rearrange("p l d -> p (l d)")

                pe.wait_ge(ag_lo, k + 1)
                split_product(pR, wc(0, 0), wc(1, 0), ag[0], ag[1], False, True).then_inc(r_mm, 1)
                if s > 0:
                    pe.wait_ge(u_v, k)
                split_product(pIN, wc(0, 2), wc(1, 2), ag[0], ag[1], True, True).then_inc(in_mm, 1)
                split_product(pZ, wc(0, 1), wc(1, 1), ag[0], ag[1], False, True).then_inc(z_mm, 1)

            def back(k, s):
                pe.wait_ge(h_v, k + 1)
                if s > LAST:
                    pe.wait_ge(f_ym, k - LAST)
                for i in range(NI):
                    last = nc.tensor.transpose(pF[:, i * P:(i + 1) * P], HF[:, s % 2, i * P:(i + 1) * P], IDF[:, :])
                last.then_inc(f_mm, 1)

            def iteration(k, s):
                if s + 1 < K:
                    aggregate(k + 1, s + 1)
                if s + 2 < K:
                    transpose_step(k + 2, s + 2)
                if s < K:
                    gates(k, s, lambda: back(k - 2, s - 2) if s - 2 >= LAST else None)
                elif s - 2 < K:
                    back(k - 2, s - 2)

            transpose_step(0, 0)
            transpose_step(1, 1)
            pe.wait_ge(prep_v, 2)
            for l in range(L):
                bank = (pR, pZ)[l % 2]
                if l >= 2:
                    pe.wait_ge(wsplit_l, l - 1)
                mm(bank[:, 0:3 * D], WLT[:, l, :], WIT, start=True, stop=True).then_inc(prep_t, 1)
            pe.wait_ge(wsplit_l, L)
            aggregate(0, 0)
            walk(pe, iteration)

            banks_a, banks_s, banks_d = (pAG, pF), (pHN, pIN), (pT[:, 0, :], pT[:, 1, :])

            def conv_a(g):
                if g >= 2:
                    pe.wait_ge(c_ae, g - 1)
                bank = banks_a[g % 2]
                for c in range(NC):
                    last = mm(bank[:, c * P:(c + 1) * P], X1[:, c, :],
                              BD[:, g, c, :, :].rearrange("p q n -> p (q n)"), start=True, stop=True)
                last.then_inc(c_a, 1)

            def conv_b(g):
                pe.wait_ge(c_ae, g + 1)
                for j, bank in enumerate((pR, pZ)):
                    if g >= 1:
                        pe.wait_ge(c_be, NH * (g - 1) + j + 1)
                    mm(bank[:, :], W1S[:, g, j * P:(j + 1) * P], YT[:, g, :], start=True, stop=True).then_inc(c_b, 1)

            def conv_s(g):
                pe.wait_ge(c_be, NH * (g + 1))
                if g >= 2:
                    pe.wait_ge(c_se, g - 1)
                bank = banks_s[g % 2]
                for c in range(NC):
                    for j in range(NH):
                        last = mm(bank[:, c * P:(c + 1) * P], H1[:, g, j, c * P:(c + 1) * P], W2S[:, g, j, :],
                                  start=(j == 0), stop=(j == NH - 1))
                last.then_inc(c_s, 1)

            def conv_d(g):
                pe.wait_ge(c_se, g + 1)
                if g >= 2:
                    pe.wait_ge(c_u, g - 1)
                bank = banks_d[g % 2]
                for c in range(NC):
                    last = mm(bank[:, c * P:(c + 1) * P], BD[:, g, c, :, :].rearrange("p q n -> p (q n)"),
                              S2[:, g, c, :], start=True, stop=True)
                last.then_inc(c_d, 1)

            pe.wait_ge(ld_g, 48)
            pe.wait_ge(bd_p, BD_STEPS)
            pe.wait_ge(f_nb, B)
            for t in range(G + 4):
                for fn, lag in ((conv_a, 0), (conv_b, 1), (conv_s, 2), (conv_d, 3)):
                    if 0 <= t - lag < G:
                        fn(t - lag)

        @block.scalar
        def _(act):
            def natural_hi(k, s):
                act.wait_ge(ld_x[s % 4], 16 * (quarter(k) + 1))
                if s >= 2:
                    act.wait_ge(ag_mm, k - 1)
                nc.scalar.activation(NAT[:, s % 2, 0, :, :], XS[:, s % 4, :, :], ACT.Copy).then_inc(nat_hi, 1)

            def evacuate_transpose(k, s):
                act.wait_ge(t_mm, k + 1)
                if s < B:
                    dst = HT[:, one(graph_of(k)), :, :].rearrange("p b h n -> p (b h) n")
                else:
                    act.wait_ge(ag_mm, k - 1)
                    dst = NAT[:, s % 2, :, :, :].rearrange("p h i d -> p h (i d)")
                nc.scalar.activation(dst, pT[:, :, :], ACT.Copy).then_inc(t_ev, 1)

            def aggregated_hi(k, s):
                act.wait_ge(ag_mm, k + 1)
                if s >= 2:
                    act.wait_ge(z_mm, k - 1)
                nc.scalar.activation(AG[:, s % 2, 0, :], pAG[:, :], ACT.Copy).then_inc(ag_hi, 1)

            def state_hi(k, s):
                act.wait_ge(h_v, k + 1)
                b = graph_of(k)
                nc.scalar.activation(HT[:, one(b), 0, :], H[:, one(b), :], ACT.Copy).then_inc(h_hi, 1)

            def normalise(k, s):
                act.wait_ge(f_nb, k - LAST + 1)
                w = s % 4
                for i in range(NI):
                    last = nc.scalar.activation(Y[:, s % 4, i, :], Y[:, s % 4, i, :], ACT.Identity,
                                                bias=NB[:, w, i:i + 1], scale=RS[:, w, i:i + 1])
                last.then_inc(f_on, 1)

            def iteration(k, s):
                if s + 1 < K:
                    aggregated_hi(k + 1, s + 1)
                if s + 2 < K:
                    evacuate_transpose(k + 2, s + 2)
                if s + 3 < B:
                    natural_hi(k + 3, s + 3)
                if LAST <= s - 5 < K:
                    normalise(k - 5, s - 5)
                if s < K:
                    act.wait_ge(r_mm, k + 1)
                    if s > 0:
                        act.wait_ge(t_v, k)
                    nc.scalar.activation(R[:, :], pR[:, :], ACT.Sigmoid, bias=BRZ[:, 0:1], scale=UNSCALE)\
                        .then_inc(sig_r, 1)
                    if 0 <= s - 1 < LAST:
                        state_hi(k - 1, s - 1)
                    act.wait_ge(z_mm, k + 1)
                    if s > 0:
                        act.wait_ge(e_v, k)
                    nc.scalar.activation(Z[:, :], pZ[:, :], ACT.Sigmoid, bias=BRZ[:, 1:2], scale=UNSCALE)\
                        .then_inc(sig_z, 1)
                    act.wait_ge(u_v, k + 1)
                    if s > 0:
                        act.wait_ge(h_v, k)
                    nc.scalar.activation(NN[:, :], T[:, :], ACT.Tanh, bias=BI[:, 2:3], scale=UNSCALE)\
                        .then_inc(n_a, 1)

            natural_hi(0, 0)
            natural_hi(1, 1)
            evacuate_transpose(0, 0)
            evacuate_transpose(1, 1)
            aggregated_hi(0, 0)
            natural_hi(2, 2)
            act.wait_ge(fw_max, 1)
            nc.scalar.activation(FW[:, :], FW[:, :], ACT.Exp, bias=FS[:, 0:1], scale=1.0).then_inc(prep_a, 1)
            act.wait_ge(wsplit_l, L)
            walk(act, iteration)

            for t in range(G + 4):
                if 0 <= t - 1 < G:
                    g = t - 1
                    for j, bank in enumerate((pR, pZ)):
                        act.wait_ge(c_b, NH * g + j + 1)
                        nc.scalar.activation(H1[:, g, j, :], bank[:, :], ACT.Relu, bias=B1[:, g, j:j + 1])\
                            .then_inc(c_be, 1)
                if 0 <= t - 2 < G:
                    g = t - 2
                    act.wait_ge(c_s, g + 1)
                    nc.scalar.activation(S2[:, g, :, :].rearrange("p c e -> p (c e)"), (pHN, pIN)[g % 2][:, :],
                                         ACT.Copy).then_inc(c_se, 1)

        @block.vector
        def _(dve):
            v = nc.vector
            links = [0]

            def link(ins):
                links[0] += 1
                ins.then_inc(chain, 1)
                dve.wait_ge(chain, links[0])

            def cast_adjacency(k, s):
                dve.wait_ge(ld_a[s % 2], 16 * (half(k) + 1))
                v.tensor_scalar(A16[:, one(graph_of(k)), :, :].rearrange("p b i n -> p (b i n)"),
                                AS[:, s % 2, :, :].rearrange("p i n -> p (i n)"), 0.0, None,
                                ALU.not_equal).then_inc(a_cast, 1)

            def aggregated_lo(k, s):
                dve.wait_ge(ag_hi, k + 1)
                v.tensor_tensor(AG[:, s % 2, 1, :], pAG[:, :], AG[:, s % 2, 0, :], ALU.subtract).then_inc(ag_lo, 1)

            dve.wait_ge(prep_t, 1)
            v.tensor_copy(WIT, pR[:, 0:3 * D])
            whh = pZ[:, 0:3 * D].rearrange("p (g d) -> p g d", g=3)
            link(v.tensor_scalar(WH[:, 0, :, :], whh, WSCALE, None, ALU.mult))
            v.scalar_tensor_tensor(out=WH[:, 1, :, :], in0=whh, scalar=WSCALE, in1=WH[:, 0, :, :],
                                   op0=ALU.mult, op1=ALU.subtract)
            dve.wait_ge(prep_t, 2)
            v.tensor_copy(WLT[:, 0:4, :].rearrange("p l d -> p (l d)"), pIN[:, :]).then_inc(prep_v, 1)
            v.tensor_copy(WLT[:, 4, :], pHN[:, 0:D]).then_inc(prep_v, 1)
            dve.wait_ge(prep_t, 3)
            link(v.tensor_copy(COLS[:, :], pF[:, 0:COLS.shape[1]]))
            v.tensor_tensor(BRZ[:, :], BI[:, 0:2], BH[:, 0:2], ALU.add)
            v.tensor_scalar(BHN[:, :], BH[:, 2:3], WSCALE, None, ALU.mult)
            cast_adjacency(0, 0)
            for l in range(L):
                dve.wait_ge(prep_t, 4 + l)
                src = (pR, pZ)[l % 2][:, 0:3 * D].rearrange("p (g d) -> p g d", g=3)
                link(v.tensor_scalar(WC[:, l, 0, :, :], src, WSCALE, None, ALU.mult))
                v.scalar_tensor_tensor(out=WC[:, l, 1, :, :], in0=src, scalar=WSCALE, in1=WC[:, l, 0, :, :],
                                       op0=ALU.mult, op1=ALU.subtract).then_inc(wsplit_l, 1)
            aggregated_lo(0, 0)
            cast_adjacency(1, 1)
            cast_adjacency(2, 2)
            for q in range(Q):
                v.tensor_copy(I32[S * q:S * q + S, :], IDF[S * q:S * q + S, S * q:S * q + S])
            dve.wait_ge(ld_f, 16)
            link(v.tensor_reduce(FS[:, 1:2], FW[:, :], AX_X, ALU.max))
            v.tensor_scalar(FS[:, 0:1], FS[:, 1:2], -1.0, None, ALU.mult).then_inc(fw_max, 1)
            dve.wait_ge(prep_a, 1)
            link(v.tensor_reduce(FS[:, 2:3], FW[:, :], AX_X, ALU.add))
            link(v.reciprocal(FS[:, 3:4], FS[:, 2:3]))
            link(v.tensor_scalar(FW[:, :], FW[:, :], FS[:, 3:4], None, ALU.mult))
            def iteration(k, s):
                if 0 <= s - 1 < K:
                    j, b = k - 1, graph_of(k - 1)
                    h_in = H[:, one(b), :]
                    h_out = H[:, one(b), :] if s - 1 < LAST else HF[:, (s - 1) % 2, :]
                    if s - 1 < LAST:
                        dve.wait_ge(n_a, j + 1)
                    if s < B - 1:
                        dve.wait_ge(hm, B if s == B - 2 else j + 1)
                    if s - 1 < LAST:
                        v.tensor_tensor(E[:, :], h_in, NN[:, :], ALU.subtract).then_inc(d_v, 1)
                if s + 1 < K:
                    aggregated_lo(k + 1, s + 1)
                if 0 <= s - 1 < K:
                    dve.wait_ge(d_v, j + 1)
                    dve.wait_ge(sig_z, j + 1)
                    v.tensor_tensor(E[:, :], E[:, :], Z[:, :], ALU.mult).then_inc(e_v, 1)
                if s + 3 < B:
                    cast_adjacency(k + 3, s + 3)
                if 0 <= s - 1 < K:
                    dve.wait_ge(e_v, j + 1)
                    if s - 1 >= LAST + 2:
                        dve.wait_ge(f_mm, j - LAST - 1)
                    v.tensor_tensor(h_out, E[:, :], NN[:, :], ALU.add).then_inc(h_v, 1)
                if LAST <= s - 2 < K:
                    f = k - 2 - LAST
                    dve.wait_ge(f_mm, f + 1)
                    if s - 2 > LAST:
                        dve.wait_ge(f_y, f)
                    v.tensor_tensor(YM[:, :, :], pF[:, :].rearrange("p (i d) -> p i d", i=NI),
                                    MASK[:, one(f), :].rearrange("p b i -> p i b").to_broadcast([P, NI, D]), ALU.mult).then_inc(f_ym, 1)
                if LAST <= s - 3 < K:
                    f = k - 3 - LAST
                    dve.wait_ge(f_y, f + 1)
                    for i in range(NI):
                        last = v.bn_stats(ST[:, i, :], Y[:, (s - 3) % 4, i, :])
                    last.then_inc(f_st, 1)
                    dve.wait_ge(f_st, f + 1)
                if LAST <= s - 4 < K:
                    f, w, n = k - 4 - LAST, (s - 4) % 4, (s - 4) % 4
                    dve.wait_ge(f_rs, f + 1)
                    v.scalar_tensor_tensor(out=NB[:, w, :], in0=MV[:, w, :, 0], scalar=-1.0, in1=RS[:, w, 0:NI],
                                           op0=ALU.mult, op1=ALU.mult)
                    v.tensor_scalar(X1[S * n:S * n + S, one(quarter(f)), :], Y[0:S, n, 0:1, :],
                                    MV[0:S, w, 0, 0:1], RS[0:S, w, NI:NI + 1],
                                    ALU.subtract, ALU.mult).then_inc(f_nb, 1)
                if LAST <= s - 3 < K:
                    f, w = k - 3 - LAST, (s - 3) % 4
                    for i in range(NI):
                        last = v.bn_aggr(MV[:, w, i, :], ST[:, i, :])
                    last.then_inc(f_mv, 1)
                    dve.wait_ge(f_mv, f + 1)
                    v.tensor_scalar(VE[:, w, 0:NI], MV[:, w, :, 1], 1.0 + EPS, EPS * EPS, ALU.mult, ALU.add)
                    v.tensor_scalar(VE[:, w, NI:NI + 1], MV[:, w, 0:1, 1], EPS, None, ALU.add).then_inc(f_var, 1)
                if s < K:
                    dve.wait_ge(sig_r, k + 1)
                    if s > 0:
                        dve.wait_ge(n_a, k)
                    v.scalar_tensor_tensor(out=T[:, :], in0=pHN[:, :], scalar=BHN[:, 0:1], in1=R[:, :],
                                           op0=ALU.add, op1=ALU.mult).then_inc(t_v, 1)
                if 0 <= s - 1 < LAST:
                    b = graph_of(k - 1)
                    dve.wait_ge(h_hi, k)
                    v.tensor_tensor(HT[:, one(b), 1, :], H[:, one(b), :], HT[:, one(b), 0, :],
                                    ALU.subtract).then_inc(h_lo, 1)
                if s < K:
                    dve.wait_ge(t_v, k + 1)
                    dve.wait_ge(in_mm, k + 1)
                    v.tensor_tensor(T[:, :], pIN[:, :], T[:, :], ALU.add).then_inc(u_v, 1)

            def sum_degrees():
                dve.wait_ge(am_p, 1)
                link(v.tensor_reduce(DG[0], AMF, AX_X, ALU.add))
                link(v.tensor_scalar(DG[2], DG[0], 0.0, None, ALU.is_equal))
                v.tensor_tensor(DG[0], DG[0], DG[2], ALU.add)
                link(v.tensor_scalar(DG[1], DG[2], -1.0, 1.0, ALU.mult, ALU.add))
                v.tensor_copy(DG[2], DG[1]).then_inc(deg_v, 1)

            def transpose_adjacency():
                dve.wait_ge(am_p, 2)
                v.transpose(AT.rearrange("p g c m -> p (g c m)").bitcast(U32),
                            AM.rearrange("p g c m -> p (g c m)").bitcast(U32)).then_inc(deg_v, 1)
                link(v.transpose(CMT[:, :, :].bitcast(U32).rearrange("p g s -> p (g s)"),
                                 CM[:, :, :].bitcast(U32).rearrange("p g s -> p (g s)")))
                v.tensor_tensor(MS[:, :], FW[:, :], CMT[:, :, 0], ALU.mult)

            walk(dve, iteration, {63: sum_degrees, 64: transpose_adjacency})

            for t in range(G + 4):
                if 0 <= t < G:
                    dve.wait_ge(c_a, t + 1)
                    v.tensor_copy(YT[:, t, :], (pAG, pF)[t % 2][:, :]).then_inc(c_ae, 1)
                if 0 <= t - 3 < G:
                    g = t - 3
                    dve.wait_ge(c_d, g + 1)
                    u = U[:, g % 2, :, :]
                    v.tensor_tensor(u, pT[:, g % 2, :].rearrange("p (c e) -> p c e", c=NC),
                                    B2S[:, g:g + 1, :].to_broadcast([P, NC, D]), ALU.add).then_inc(c_u, 1)
                    dve.wait_ge(c_u, g + 1)
                    v.tensor_scalar(u, u, 0.0, MS[:, g:g + 1], ALU.max, ALU.mult).then_inc(c_m, 1)
                    dve.wait_ge(c_m, g + 1)
                    if g > 0:
                        dve.wait_ge(c_f, g)
                    v.tensor_tensor(FU, X1[:, :, :] if g == 0 else FU, u, ALU.add).then_inc(c_f, 1)
            dve.wait_ge(c_f, G)
            for c in range(NC):
                last = v.bn_stats(ST[:, c, :], FU[:, c, :])
            last.then_inc(z_v, 1)
            dve.wait_ge(z_v, 1)
            for c in range(NC):
                last = v.bn_aggr(MV[:, 0, c, :], ST[:, c, :])
            last.then_inc(z_v, 1)
            dve.wait_ge(z_v, 2)
            v.tensor_scalar(VE[:, 0, 0:NC], MV[:, 0, :, 1], EPS, None, ALU.add).then_inc(z_v, 1)
            dve.wait_ge(z_p, 1)
            for c in range(NC):
                last = v.tensor_scalar(ZO[:, c, :], FU[:, c, :], MV[:, 0, c, 0:1], RS[:, 0, c:c + 1],
                                       ALU.subtract, ALU.mult)
            last.then_inc(z_o, 1)


_INS = ['x', 'adj', 'nodemask', 'L0_gnn_weight', 'L0_gnn_w_ih', 'L0_gnn_w_hh', 'L0_gnn_b_ih', 'L0_gnn_b_hh',
        'L1_gnn_W1', 'L1_gnn_b1', 'L1_gnn_W2', 'L1_gnn_b2', 'L1_gnn_fusion_w']


def kernel(**inputs):
    import numpy as _np
    import concourse.bacc as _bacc
    from concourse.bass_utils import run_bass_kernel_spmd as _run

    nc = _bacc.Bacc("TRN2", target_bir_lowering=False, num_devices=1)
    arrays, args = {}, []
    for name in _INS:
        a = _np.ascontiguousarray(inputs[name])
        arrays[f"in_{name}_dram"] = a
        args.append(nc.dram_tensor(f"in_{name}_dram", a.shape, mybir.dt.from_np(a.dtype), kind="ExternalInput").ap())
    args.append(nc.dram_tensor("out_dram", (B, N, D), F32, kind="ExternalOutput").ap())
    graph_net_kernel(nc, *args)
    r = _run(nc, [arrays], core_ids=[0])
    return r.results[0]["out_dram"]
```

```python
from contextlib import ExitStack

import concourse.bass as bass
from concourse import mybir

ALU = mybir.AluOpType
ACT = mybir.ActivationFunctionType
AX_X = mybir.AxisListType.X
F32 = mybir.dt.float32
F16 = mybir.dt.float16
U32 = mybir.dt.uint32

P = 128
B, N, D = 16, 512, 128
L = 5
NI = N // P
K = B * L
LAST = K - B
GROUPS = [list(range(25)), [0, 1, 2, 3, 4, 5, 6, 7, 8], [0, 9, 10, 11, 12, 13, 14],
          [6, 7, 8, 12, 13, 14], [3, 4, 5, 9, 10, 11]]
G = len(GROUPS)
HID = 256
NH = HID // P
Q = 4
S = P // Q
NC = B // Q
EPS = 1e-5
WSCALE = 1024.0
UNSCALE = 1.0 / WSCALE

MIDDLE = (14, 62)
SEGMENTS = [0, (1, 13), 13, MIDDLE, 62, 63, 64, 65, 66, 67, 68, (69, 77), 77, 78, 79]
TAIL = [80, 81, 82, 83, 84]


def walk(eng, iteration, before=None):
    for seg in SEGMENTS:
        if isinstance(seg, int):
            if before and seg in before:
                before[seg]()
            iteration(seg, seg)
        else:
            with eng.Fori(seg[0], seg[1] - 3, 4) as k0:
                for j in range(4):
                    iteration(k0 + j, seg[0] + j)
    for k in TAIL:
        iteration(k, k)


def graph_of(k):
    return k % B if isinstance(k, int) else (k & (B - 1))


def layer_of(k):
    return k // B if isinstance(k, int) else (k >> 4)


def half(k):
    return k // 2 if isinstance(k, int) else (k >> 1)


def quarter(k):
    return k // 4 if isinstance(k, int) else (k >> 2)


def runs_of(members):
    runs = []
    for m in members:
        if runs and runs[-1][-1] == m - 1:
            runs[-1].append(m)
        else:
            runs.append([m])
    return runs


def one(i):
    return slice(i, i + 1) if isinstance(i, int) else bass.ds(i, 1)


def graph_net_kernel(nc, x, adj, nodemask, weight, w_ih, w_hh, b_ih, b_hh, W1, b1, W2, b2, fusion_w, out):
    ctx = ExitStack()
    with ctx:
        def sb(name, shape, dt):
            return ctx.enter_context(nc.sbuf_tensor(name, shape, dt))

        def pb(name, shape):
            return ctx.enter_context(nc.psum_tensor(name, shape, F32))

        def sem(name):
            return ctx.enter_context(nc.semaphore(name))

        A16 = sb("A16", [P, B, NI, N], F16)
        HT = sb("HT", [P, B, 2, N], F16)
        H = sb("H", [P, B, N], F32)
        AS = sb("AS", [P, 2, NI, N], F32)
        XS = sb("XS", [P, 4, NI, D], F32)
        NAT = sb("NAT", [P, 2, 2, NI, D], F16)
        AG = sb("AG", [P, 2, 2, N], F16)
        HF = sb("HF", [P, 2, N], F32)
        Y = sb("Y", [P, 4, NI, D], F32)
        R = sb("R", [P, N], F32)
        Z = sb("Z", [P, N], F32)
        T = sb("T", [P, N], F32)
        NN = sb("NN", [P, N], F32)
        E = sb("E", [P, N], F32)
        WC = sb("WC", [P, L, 2, 3, D], F16)
        WH = sb("WH", [P, 2, 3, D], F16)
        BRZ = sb("BRZ", [P, 2], F32)
        BHN = sb("BHN", [P, 1], F32)
        IDF = sb("IDF", [P, P], F32)
        I32 = sb("I32", [P, S], F32)
        rows_m, rows_i, rows_h, rows_1 = 0, B * NI, B * NI + 3, B * NI + 6
        ROWS = sb("ROWS", [rows_1 + G * NH, P], F32)
        COLS = sb("COLS", [P, rows_1 + G * NH], F32)
        MASK = COLS[:, 0:rows_i].rearrange("p (b i) -> p b i", b=B)
        BI = COLS[:, rows_i:rows_h]
        BH = COLS[:, rows_h:rows_1]
        B1 = COLS[:, rows_1:].rearrange("p (g j) -> p g j", g=G)
        ST = sb("ST", [P, NI, 6], F32)
        MV = sb("MV", [P, 4, NI, 2], F32)
        VE = sb("VE", [P, 4, NI + 1], F32)
        RS = sb("RS", [P, 4, NI + 1], F32)
        NB = sb("NB", [P, 4, NI], F32)
        NHALF = sb("NHALF", [P, G * NC], F32)
        BD = sb("BD", [P, G, NC, Q, S], F32)
        X1 = sb("X1", [P, NC, D], F32)
        CM = sb("CM", [P, G, S], F32)
        CMT = sb("CMT", [P, G, S], F32)
        FW = sb("FW", [P, G], F32)
        FS = sb("FS", [P, 4], F32)
        MS = sb("MS", [P, G], F32)
        DEG = sb("DEG", [P, 3, G * NC], F32)
        DG = [DEG[:, i, :] for i in range(3)]

        scr = A16[:, B - 4:B, :, :].rearrange("p b i n -> p (b i n)").bitcast(F32)
        off = [0]

        def scratch(n):
            off[0] += n
            assert off[0] <= 4 * NI * N // 2
            return scr[:, off[0] - n:off[0]]

        WL = scratch(L * D).rearrange("p (l e) -> p l e", l=L)
        WLT = scratch(L * D).rearrange("p (l e) -> p l e", l=L)
        WI = scratch(3 * D).rearrange("p (g e) -> p g e", g=3)
        WHS = scratch(3 * D).rearrange("p (g e) -> p g e", g=3)
        WIT = scratch(3 * D)
        y_flat = Y[:, :, :, :].rearrange("p s i d -> p (s i d)")
        y_end = G * NC * S
        AM = y_flat[:, 0:y_end].rearrange("p (g c m) -> p g c m", g=G, c=NC)
        AT = y_flat[:, y_end:2 * y_end].rearrange("p (g c m) -> p g c m", g=G, c=NC)
        AB = y_flat[:, 2 * y_end:2 * y_end + NC * S].rearrange("p (c m) -> p c m", c=NC)
        AMF = y_flat[:, 0:y_end].rearrange("p (x m) -> p x m", m=S)

        as_flat = AS[:, :, :, :].rearrange("p s i n -> p (s i n)")
        W1S = as_flat[:, 0:G * HID].rearrange("p (g e) -> p g e", g=G)
        W2S = as_flat[:, G * HID:2 * G * HID].rearrange("p (g j e) -> p g j e", g=G, j=NH)
        B2S = as_flat[:, 2 * G * HID:2 * G * HID + G * D].rearrange("p (g e) -> p g e", g=G)
        w_end = 2 * G * HID + G * D
        YM = as_flat[:, w_end:w_end + NI * D].rearrange("p (i d) -> p i d", i=NI)
        lateA = A16[:, :, :, :].rearrange("p b i n -> p (b i n)").bitcast(F32)
        YT = lateA[:, 0:G * N].rearrange("p (g n) -> p g n", g=G)
        H1 = lateA[:, G * N:3 * G * N].rearrange("p (g j n) -> p g j n", g=G, j=NH)
        S2 = lateA[:, 3 * G * N:4 * G * N].rearrange("p (g c e) -> p g c e", g=G, c=NC)
        U = lateA[:, 4 * G * N:(4 * G + 2) * N].rearrange("p (s c e) -> p s c e", s=2, c=NC)
        FU = lateA[:, (4 * G + 2) * N:(4 * G + 3) * N].rearrange("p (c e) -> p c e", c=NC)
        ZO = lateA[:, (4 * G + 3) * N:(4 * G + 4) * N].rearrange("p (c e) -> p c e", c=NC)

        pAG = pb("pAG", [P, N])
        pR = pb("pR", [P, N])
        pZ = pb("pZ", [P, N])
        pIN = pb("pIN", [P, N])
        pHN = pb("pHN", [P, N])
        pF = pb("pF", [P, N])
        pA2 = pb("pA2", [P, 2, N])

        MERGE = (pR, pF, pHN)

        ld_x = [sem(f"ld_x{i}") for i in range(4)]
        ld_a = [sem(f"ld_a{i}") for i in range(2)]
        ld_w = sem("ld_w")
        ld_r = sem("ld_r")
        ld_c = sem("ld_c")
        ld_f = sem("ld_f")
        ld_g = sem("ld_g")
        st_y = [sem(f"st_y{i}") for i in range(4)]
        st_z = sem("st_z")
        ident = sem("ident")
        masks0 = sem("masks0")
        prep_t = sem("prep_t")
        prep_v = sem("prep_v")
        prep_a = sem("prep_a")
        wsplit_l = sem("wsplit_l")
        w_hi = sem("w_hi")
        cols_v = sem("cols_v")
        fw_max = sem("fw_max")
        chain = sem("chain")
        deg_v = sem("deg_v")
        BD_STEPS = 4 + Q
        bd_p = sem("bd_p")
        am_p = sem("am_p")
        nat_hi = sem("nat_hi")
        nat_lo = sem("nat_lo")
        a_cast = sem("a_cast")
        turn = [sem(f"turn{i}") for i in range(2)]
        hm = sem("hm")
        ag_mm = sem("ag_mm")
        ag_hi = sem("ag_hi")
        ag_lo = sem("ag_lo")
        r_mm = sem("r_mm")
        in_mm = sem("in_mm")
        z_mm = sem("z_mm")
        sig_r = sem("sig_r")
        sig_z = sem("sig_z")
        t_v = sem("t_v")
        u_v = sem("u_v")
        n_a = sem("n_a")
        d_v = sem("d_v")
        e_v = sem("e_v")
        h_v = sem("h_v")
        h_hi = sem("h_hi")
        h_lo = sem("h_lo")
        f_mm = sem("f_mm")
        f_ym = sem("f_ym")
        f_y = sem("f_y")
        f_st = sem("f_st")
        f_mv = sem("f_mv")
        f_var = sem("f_var")
        f_rs = sem("f_rs")
        f_nb = sem("f_nb")
        f_on = sem("f_on")
        c_a = sem("c_a")
        c_ae = sem("c_ae")
        c_b = sem("c_b")
        c_be = sem("c_be")
        c_s = sem("c_s")
        c_se = sem("c_se")
        c_d = sem("c_d")
        c_u = sem("c_u")
        c_m = sem("c_m")
        c_f = sem("c_f")
        z_v = sem("z_v")
        z_p = sem("z_p")
        z_o = sem("z_o")

        block = ctx.enter_context(nc.Block())

        @block.sync
        def _(sp):
            def load_x(slot, b):
                sp.dma_start(XS[:, slot, :, :],
                             x[one(b), :, :].rearrange("b (i p) d -> p (b i) d", p=P)).then_inc(ld_x[slot], 16)

            def load_a(slot, b):
                sp.dma_start(AS[:, slot, :, :],
                             adj[one(b), :, :].rearrange("b (i p) n -> p (b i) n", p=P)).then_inc(ld_a[slot], 16)

            sp.dma_start(WI, w_ih.rearrange("(g c) d -> c g d", c=P)).then_inc(ld_w, 16)
            sp.dma_start(WHS, w_hh.rearrange("(g c) d -> c g d", c=P)).then_inc(ld_w, 16)
            sp.dma_start(WL, weight.rearrange("l d e -> d l e")).then_inc(ld_w, 16)
            load_a(0, 0)
            for row, src in ((rows_m, nodemask.rearrange("b (i p) -> (b i) p", p=P)),
                             (rows_i, b_ih.rearrange("(g p) -> g p", p=P)),
                             (rows_h, b_hh.rearrange("(g p) -> g p", p=P)),
                             (rows_1, b1.rearrange("g (j p) -> (g j) p", p=P))):
                sp.dma_start(ROWS[row:row + src.shape[0], :], src).then_inc(ld_r, 16)
            load_x(2, 2)
            load_x(3, 3)
            load_a(1, 1)

            def transpose_x(b, s):
                sp.wait_ge(nat_lo, b + 1)
                sp.dma_start_transpose(HT[:, one(b), :, :].rearrange("p b h (i n) -> p (b h i) n", i=NI),
                                       NAT[:, s % 2, :, :, :].rearrange("p h i d -> p (h i d)"))\
                    .then_inc(turn[s % 2], 16)

            def transpose_h(k, s, b):
                sp.wait_ge(ag_mm, k - 1)
                sp.dma_start_transpose(NAT[:, s % 2, :, :, :].rearrange("p h i d -> p (h i) d"),
                                       HT[:, one(b), :, :].rearrange("p b h n -> p (b h n)"))\
                    .then_inc(turn[s % 2], 16)

            def next_a(k, s):
                sp.wait_ge(a_cast, k - 1)
                load_a(s % 2, k)

            def next_x(k, s):
                sp.wait_ge(nat_lo, k - 3)
                load_x(s % 4, k)

            def late_loads():
                for b in range(4):
                    sp.wait_ge(nat_lo, B - 3 + b)
                    load_x(b, b)
                for q in range(Q):
                    sp.dma_start(AB[S * q:S * q + S, :, :],
                                 adj.rearrange("(c q) n m -> q n c m", q=Q)[q, 0:S, :, 0:S]).then_inc(ld_c, 16)
                sp.wait_ge(a_cast, B)
                sp.dma_start(W1S, W1.rearrange("g d e -> d g e")).then_inc(ld_g, 16)
                sp.dma_start(W2S, W2.rearrange("g (j h) e -> h g j e", j=NH)).then_inc(ld_g, 16)
                sp.dma_start(B2S, b2.partition_broadcast(P)).then_inc(ld_g, 16)

            def store_y(b, slot):
                sp.wait_ge(f_on, b + 1)
                sp.dma_start(out[one(b), S:P, :].rearrange("b p d -> p (b d)"),
                             Y[S:P, slot, 0, :]).then_inc(st_y[slot], 16)
                sp.dma_start(out[one(b), P:N, :].rearrange("b (i p) d -> p (b i) d", p=P),
                             Y[:, slot, 1:NI, :]).then_inc(st_y[slot], 16)

            def next_x_again(f, slot):
                sp.wait_ge(st_y[slot], 32 * (quarter(f) + 1))
                load_x(slot, f + 4)

            transpose_x(0, 0)
            transpose_x(1, 1)
            for b in range(2, 5):
                next_a(b, b)
            for b in range(4, 6):
                next_x(b, b)
            for b in range(2, 4):
                transpose_x(b, b)
                next_a(b + 3, b + 3)
                next_x(b + 4, b + 4)
            with sp.Fori(4, 9, 4) as b0:
                for j in range(4):
                    transpose_x(b0 + j, j)
                    next_a(b0 + j + 3, j + 3)
                    next_x(b0 + j + 4, j + 4)
            for b in range(12, B):
                transpose_x(b, b)
                if b + 3 < B:
                    next_a(b + 3, b + 3)
            for i in range(2):
                sp.wait_ge(turn[i], 16 * (B // 2))
            with sp.Fori(1, L - 1) as l:
                with sp.Fori(0, B - 3, 4) as b0:
                    for j in range(4):
                        transpose_h(l * B + b0 + j, j, b0 + j)
            late_loads()
            with sp.Fori(0, 5, 4) as b0:
                for j in range(4):
                    transpose_h(b0 + LAST + j, j, b0 + j)
            with sp.Fori(8, B - 3, 4) as b0:
                for j in range(4):
                    transpose_h(b0 + LAST + j, j, b0 + j)
                    store_y(b0 - 8 + j, j)
                    next_x_again(b0 - 8 + j, j)
            for f in range(8, B):
                store_y(f, f % 4)
                if f + 4 < B:
                    next_x_again(f, f % 4)
            for q in range(Q):
                sp.wait_ge(z_o, 1)
                sp.dma_start(out.rearrange("(c q) n d -> q n c d", q=Q)[q, 0:S],
                             ZO[S * q:S * q + S, :, :]).then_inc(st_z, 16)
            for slot in range(4):
                sp.wait_ge(st_y[slot], 32 * (B // 4))
            sp.wait_ge(st_z, 16 * Q)

        @block.gpsimd
        def _(pool):
            nc.gpsimd.memset(IDF[:, :], 0.0).then_inc(ident, 1)
            pool.wait_ge(ident, 1)
            nc.gpsimd.affine_select(out=IDF[:, :], in_=IDF[:, :], compare_op=ALU.not_equal, fill=1.0,
                                    base=0, pattern=[[-1, P]], channel_multiplier=1).then_inc(ident, 1)
            nc.gpsimd.memset(NHALF[:, :], -0.5)
            nc.gpsimd.memset(CM[:, :, :], 0.0).then_inc(masks0, 1)
            pool.wait_ge(masks0, 1)
            for g, members in enumerate(GROUPS):
                for run in runs_of(members):
                    last = nc.gpsimd.memset(CM[:, g, run[0]:run[-1] + 1], 1.0)
            last.then_inc(masks0, 1)
            def natural_lo(k, s):
                pool.wait_ge(nat_hi, k + 1)
                nc.gpsimd.tensor_tensor(NAT[:, s % 2, 1, :, :], XS[:, s % 4, :, :], NAT[:, s % 2, 0, :, :],
                                        ALU.subtract).then_inc(nat_lo, 1)

            def iteration(k, s):
                if LAST <= s - 1 < K:
                    pool.wait_ge(n_a, k)
                    pool.wait_ge(h_v, k - 1)
                    nc.gpsimd.tensor_tensor(E[:, :], H[:, one(graph_of(k - 1)), :], NN[:, :],
                                            ALU.subtract).then_inc(d_v, 1)
                if s + 3 < B:
                    natural_lo(k + 3, s + 3)
                if s + 2 < B:
                    b = graph_of(k + 2)
                    pool.wait_ge(turn[s % 2], 16 * (half(k + 2) + 1))
                    nc.gpsimd.tensor_tensor(H[:, one(b), :], HT[:, one(b), 0, :], HT[:, one(b), 1, :],
                                            ALU.add).then_inc(hm, 1)
                if LAST <= s - 2 < K:
                    f, slot = k - 2 - LAST, (s - 2) % 4
                    pool.wait_ge(f_ym, f + 1)
                    pool.wait_ge(ld_x[slot], 16 * (B // 4) + 16 * (quarter(f) + 1))
                    nc.gpsimd.tensor_tensor(Y[:, slot, :, :], YM[:, :, :], XS[:, slot, :, :],
                                            ALU.add).then_inc(f_y, 1)
                if LAST <= s - 3 < K:
                    f, w = k - 3 - LAST, (s - 3) % 4
                    pool.wait_ge(f_var, f + 1)
                    nc.gpsimd.tensor_tensor(RS[:, w, :], VE[:, w, :], NHALF[:, 0:NI + 1], ALU.pow).then_inc(f_rs, 1)

            natural_lo(0, 0)
            natural_lo(1, 1)
            natural_lo(2, 2)
            for b in range(2):
                pool.wait_ge(turn[b], 16)
                nc.gpsimd.tensor_tensor(H[:, b, :], HT[:, b, 0, :], HT[:, b, 1, :], ALU.add).then_inc(hm, 1)

            def prepare_adjacency():
                g_ = nc.gpsimd
                n = [0]

                def link(ins):
                    n[0] += 1
                    ins.then_inc(bd_p, 1)
                    pool.wait_ge(bd_p, n[0])

                pool.wait_ge(ld_c, 16 * Q)
                for g in range(G):
                    last = g_.tensor_tensor(AM[:, g, :, :], AB[:, :, :],
                                            CM[:, g:g + 1, :].to_broadcast([P, NC, S]), ALU.mult)
                link(last)
                link(g_.tensor_tensor(AMF, AMF, I32[:, None, :].to_broadcast([P, G * NC, S]), ALU.add))
                g_.memset(BD[:, :, :, :, :].rearrange("p g c q s -> p (g c q s)"), 0.0).then_inc(am_p, 1)
                pool.wait_ge(deg_v, 1)
                link(g_.tensor_tensor(DG[1], DG[0], NHALF[:, :], ALU.pow))
                link(g_.tensor_tensor(DG[2], DG[2], DG[1], ALU.mult))
                g_.tensor_tensor(AMF, AMF, DG[2][:, :, None].to_broadcast([P, G * NC, S]), ALU.mult).then_inc(am_p, 1)
                pool.wait_ge(deg_v, 2)
                pool.wait_ge(am_p, 2)
                for q in range(Q):
                    rows = slice(S * q, S * q + S)
                    link(g_.tensor_tensor(BD[rows, :, :, q, :].rearrange("p g c s -> p (g c) s"),
                                            AT[rows, :, :, :].rearrange("p g c m -> p (g c) m"),
                                            DG[2][rows, :, None].to_broadcast([S, G * NC, S]), ALU.mult))

                assert n[0] == BD_STEPS

            walk(pool, iteration, {62: prepare_adjacency})
            pool.wait_ge(z_v, 3)
            nc.gpsimd.tensor_tensor(RS[:, 0, 0:NC], VE[:, 0, 0:NC], NHALF[:, 0:NC], ALU.pow).then_inc(z_p, 1)

        @block.tensor
        def _(pe):
            mm = nc.tensor.matmul
            pe.wait_ge(ident, 2)
            pe.wait_ge(ld_w, 16 * 3)
            for g in range(3):
                nc.tensor.transpose(pR[:, g * D:(g + 1) * D], WI[:, g, :], IDF[:, :])
            last = None
            for g in range(3):
                last = nc.tensor.transpose(pZ[:, g * D:(g + 1) * D], WHS[:, g, :], IDF[:, :])
            last.then_inc(prep_t, 1)
            for l in range(4):
                nc.tensor.transpose(pIN[:, l * D:(l + 1) * D], WL[:, l, :], IDF[:, :])
            nc.tensor.transpose(pHN[:, 0:D], WL[:, 4, :], IDF[:, :]).then_inc(prep_t, 1)

            def aggregate(k, s):
                b = graph_of(k)
                if s < B - 1:
                    pe.wait_ge(nat_lo, k + 1)
                    pe.wait_ge(a_cast, k + 1)
                else:
                    if s == B - 1:
                        pe.wait_ge(nat_lo, B)
                        pe.wait_ge(a_cast, B)
                    pe.wait_ge(turn[s % 2], 16 * (half(k) + 1))
                if s > 1:
                    pe.wait_ge(ag_lo, k - 1)
                for h in range(2):
                    for i in range(NI):
                        last = mm(pA2[:, s % 2, :], NAT[:, s % 2, h, i, :], A16[:, one(b), i, :],
                                  start=(h == 0 and i == 0), stop=(h == 1 and i == NI - 1))
                last.then_inc(ag_mm, 1)

            def split_product(bank, w_hi, w_lo, v_hi, v_lo, start, stop):
                mm(bank[:, :], w_hi, v_hi, start=start, stop=False)
                mm(bank[:, :], w_hi, v_lo, start=False, stop=False)
                return mm(bank[:, :], w_lo, v_hi, start=False, stop=stop)

            def gates(k, s, between):
                b = graph_of(k)
                l = layer_of(k) if MIDDLE[0] <= s < MIDDLE[1] else s // B
                ht = [HT[:, one(b), h, :] for h in range(2)]
                pe.wait_ge(turn[s % 2], 16 * (half(k) + 1))
                if s > 0:
                    pe.wait_ge(t_v, k)
                split_product(pHN, WH[:, 0, 2, :], WH[:, 1, 2, :], ht[0], ht[1], True, True)
                if s > 0:
                    pe.wait_ge(sig_r, k)
                split_product(pR, WH[:, 0, 0, :], WH[:, 1, 0, :], ht[0], ht[1], True, False)
                if s > 0:
                    pe.wait_ge(sig_z, k)
                split_product(pZ, WH[:, 0, 1, :], WH[:, 1, 1, :], ht[0], ht[1], True, False)
                between()
                ag = [AG[:, s % 2, h, :] for h in range(2)]

                def wc(h, g):
                    if isinstance(l, int):
                        return WC[:, l, h, g, :]
                    return WC[:, one(l), h, g, :].rearrange("p l d -> p (l d)")

                pe.wait_ge(ag_lo, k + 1)
                split_product(pR, wc(0, 0), wc(1, 0), ag[0], ag[1], False, True).then_inc(r_mm, 1)
                if s > 0:
                    pe.wait_ge(u_v, k)
                split_product(pIN, wc(0, 2), wc(1, 2), ag[0], ag[1], True, True).then_inc(in_mm, 1)
                split_product(pZ, wc(0, 1), wc(1, 1), ag[0], ag[1], False, True).then_inc(z_mm, 1)

            def back(k, s):
                pe.wait_ge(h_v, k + 1)
                if s > LAST:
                    pe.wait_ge(f_ym, k - LAST)
                for i in range(NI):
                    last = nc.tensor.transpose(pF[:, i * P:(i + 1) * P], HF[:, s % 2, i * P:(i + 1) * P], IDF[:, :])
                last.then_inc(f_mm, 1)

            def iteration(k, s):
                if s + 1 < K:
                    aggregate(k + 1, s + 1)
                if s < K:
                    gates(k, s, lambda: back(k - 2, s - 2) if s - 2 >= LAST else None)
                elif s - 2 < K:
                    back(k - 2, s - 2)

            pe.wait_ge(prep_v, 1)
            for l in range(L):
                if l == 2:
                    pe.wait_ge(prep_v, 2)
                if l >= 3:
                    pe.wait_ge(wsplit_l, l - 2)
                mm(MERGE[l % 3][:, 0:3 * D], WLT[:, l, :], WIT, start=True, stop=True).then_inc(prep_t, 1)
            pe.wait_ge(ld_r, 16 * 4)
            rows = ROWS.shape[0]
            nc.tensor.transpose(pIN[:, 0:rows], ROWS[:, :], IDF[0:rows, 0:rows]).then_inc(prep_t, 1)
            aggregate(0, 0)
            pe.wait_ge(cols_v, 1)
            walk(pe, iteration)

            banks_a, banks_s, banks_d = (pAG, pF), (pHN, pIN), (pA2[:, 0, :], pA2[:, 1, :])

            def conv_a(g):
                if g >= 2:
                    pe.wait_ge(c_ae, g - 1)
                bank = banks_a[g % 2]
                for c in range(NC):
                    last = mm(bank[:, c * P:(c + 1) * P], X1[:, c, :],
                              BD[:, g, c, :, :].rearrange("p q n -> p (q n)"), start=True, stop=True)
                last.then_inc(c_a, 1)

            def conv_b(g):
                pe.wait_ge(c_ae, g + 1)
                for j, bank in enumerate((pR, pZ)):
                    if g >= 1:
                        pe.wait_ge(c_be, NH * (g - 1) + j + 1)
                    mm(bank[:, :], W1S[:, g, j * P:(j + 1) * P], YT[:, g, :], start=True, stop=True).then_inc(c_b, 1)

            def conv_s(g):
                pe.wait_ge(c_be, NH * (g + 1))
                if g >= 2:
                    pe.wait_ge(c_se, g - 1)
                bank = banks_s[g % 2]
                for c in range(NC):
                    for j in range(NH):
                        last = mm(bank[:, c * P:(c + 1) * P], H1[:, g, j, c * P:(c + 1) * P], W2S[:, g, j, :],
                                  start=(j == 0), stop=(j == NH - 1))
                last.then_inc(c_s, 1)

            def conv_d(g):
                pe.wait_ge(c_se, g + 1)
                if g >= 2:
                    pe.wait_ge(c_u, g - 1)
                bank = banks_d[g % 2]
                for c in range(NC):
                    last = mm(bank[:, c * P:(c + 1) * P], BD[:, g, c, :, :].rearrange("p q n -> p (q n)"),
                              S2[:, g, c, :], start=True, stop=True)
                last.then_inc(c_d, 1)

            pe.wait_ge(ld_g, 48)
            pe.wait_ge(bd_p, BD_STEPS)
            pe.wait_ge(f_nb, B)
            for t in range(G + 4):
                for fn, lag in ((conv_a, 0), (conv_b, 1), (conv_s, 2), (conv_d, 3)):
                    if 0 <= t - lag < G:
                        fn(t - lag)

        @block.scalar
        def _(act):
            def natural_hi(k, s):
                act.wait_ge(ld_x[s % 4], 16 * (quarter(k) + 1))
                if s >= 2:
                    act.wait_ge(ag_mm, k - 1)
                    act.wait_ge(turn[s % 2], 16 * half(k))
                nc.scalar.activation(NAT[:, s % 2, 0, :, :], XS[:, s % 4, :, :], ACT.Copy).then_inc(nat_hi, 1)

            def aggregated_hi(k, s):
                act.wait_ge(ag_mm, k + 1)
                if s >= 2:
                    act.wait_ge(z_mm, k - 1)
                nc.scalar.activation(AG[:, s % 2, 0, :], pA2[:, s % 2, :], ACT.Copy).then_inc(ag_hi, 1)

            def state_hi(k, s):
                act.wait_ge(h_v, k + 1)
                b = graph_of(k)
                nc.scalar.activation(HT[:, one(b), 0, :], H[:, one(b), :], ACT.Copy).then_inc(h_hi, 1)

            def normalise(k, s):
                act.wait_ge(f_nb, k - LAST + 1)
                w = s % 4
                for i in range(NI):
                    last = nc.scalar.activation(Y[:, s % 4, i, :], Y[:, s % 4, i, :], ACT.Identity,
                                                bias=NB[:, w, i:i + 1], scale=RS[:, w, i:i + 1])
                last.then_inc(f_on, 1)

            def iteration(k, s):
                if s + 1 < K:
                    aggregated_hi(k + 1, s + 1)
                if s + 3 < B:
                    natural_hi(k + 3, s + 3)
                if s < K:
                    act.wait_ge(r_mm, k + 1)
                    if s > 0:
                        act.wait_ge(t_v, k)
                    nc.scalar.activation(R[:, :], pR[:, :], ACT.Sigmoid, bias=BRZ[:, 0:1], scale=UNSCALE)\
                        .then_inc(sig_r, 1)
                if LAST <= s - 5 < K:
                    normalise(k - 5, s - 5)
                if s < K:
                    if 0 <= s - 1 < LAST:
                        state_hi(k - 1, s - 1)
                    act.wait_ge(z_mm, k + 1)
                    if s > 0:
                        act.wait_ge(e_v, k)
                    nc.scalar.activation(Z[:, :], pZ[:, :], ACT.Sigmoid, bias=BRZ[:, 1:2], scale=UNSCALE)\
                        .then_inc(sig_z, 1)
                    act.wait_ge(u_v, k + 1)
                    if s > 0:
                        act.wait_ge(h_v, k)
                    nc.scalar.activation(NN[:, :], T[:, :], ACT.Tanh, bias=BI[:, 2:3], scale=UNSCALE)\
                        .then_inc(n_a, 1)

            act.dma_start(FW[:, :], fusion_w.partition_broadcast(P)).then_inc(ld_f, 16)
            for b in range(2):
                act.dma_start(XS[:, b, :, :], x[b, :, :].rearrange("(i p) d -> p i d", p=P)).then_inc(ld_x[b], 16)
            act.wait_ge(fw_max, 1)
            nc.scalar.activation(FW[:, :], FW[:, :], ACT.Exp, bias=FS[:, 0:1], scale=1.0).then_inc(prep_a, 1)
            natural_hi(0, 0)
            natural_hi(1, 1)
            act.wait_ge(prep_t, 1)
            nc.scalar.activation(WH[:, 0, :, :].rearrange("p g d -> p (g d)"), pZ[:, 0:3 * D], ACT.Copy,
                                 scale=WSCALE).then_inc(w_hi, 1)
            for l in range(L):
                act.wait_ge(prep_t, 3 + l)
                nc.scalar.activation(WC[:, l, 0, :, :].rearrange("p g d -> p (g d)"), MERGE[l % 3][:, 0:3 * D],
                                     ACT.Copy, scale=WSCALE).then_inc(w_hi, 1)
            aggregated_hi(0, 0)
            natural_hi(2, 2)
            act.wait_ge(cols_v, 1)
            walk(act, iteration)

            for t in range(G + 4):
                if 0 <= t - 1 < G:
                    g = t - 1
                    for j, bank in enumerate((pR, pZ)):
                        act.wait_ge(c_b, NH * g + j + 1)
                        nc.scalar.activation(H1[:, g, j, :], bank[:, :], ACT.Relu, bias=B1[:, g, j:j + 1])\
                            .then_inc(c_be, 1)
                if 0 <= t - 2 < G:
                    g = t - 2
                    act.wait_ge(c_s, g + 1)
                    nc.scalar.activation(S2[:, g, :, :].rearrange("p c e -> p (c e)"), (pHN, pIN)[g % 2][:, :],
                                         ACT.Copy).then_inc(c_se, 1)

        @block.vector
        def _(dve):
            v = nc.vector
            links = [0]

            def link(ins):
                links[0] += 1
                ins.then_inc(chain, 1)
                dve.wait_ge(chain, links[0])

            def cast_adjacency(k, s):
                dve.wait_ge(ld_a[s % 2], 16 * (half(k) + 1))
                v.tensor_scalar(A16[:, one(graph_of(k)), :, :].rearrange("p b i n -> p (b i n)"),
                                AS[:, s % 2, :, :].rearrange("p i n -> p (i n)"), 0.0, None,
                                ALU.not_equal).then_inc(a_cast, 1)

            def aggregated_lo(k, s):
                dve.wait_ge(ag_hi, k + 1)
                v.tensor_tensor(AG[:, s % 2, 1, :], pA2[:, s % 2, :], AG[:, s % 2, 0, :], ALU.subtract).then_inc(ag_lo, 1)

            dve.wait_ge(ld_f, 16)
            link(v.tensor_reduce(FS[:, 1:2], FW[:, :], AX_X, ALU.max))
            v.tensor_scalar(FS[:, 0:1], FS[:, 1:2], -1.0, None, ALU.mult).then_inc(fw_max, 1)
            dve.wait_ge(prep_a, 1)
            link(v.tensor_reduce(FS[:, 2:3], FW[:, :], AX_X, ALU.add))
            link(v.reciprocal(FS[:, 3:4], FS[:, 2:3]))
            link(v.tensor_scalar(FW[:, :], FW[:, :], FS[:, 3:4], None, ALU.mult))
            dve.wait_ge(prep_t, 1)
            v.tensor_copy(WIT, pR[:, 0:3 * D])
            dve.wait_ge(prep_t, 2)
            v.tensor_copy(WLT[:, 0:4, :].rearrange("p l d -> p (l d)"), pIN[:, :]).then_inc(prep_v, 1)
            v.tensor_copy(WLT[:, 4, :], pHN[:, 0:D])

            def split_lo(dst_hi, dst_lo, bank):
                src = bank[:, 0:3 * D].rearrange("p (g d) -> p g d", g=3)
                return v.scalar_tensor_tensor(out=dst_lo, in0=src, scalar=WSCALE, in1=dst_hi,
                                              op0=ALU.mult, op1=ALU.subtract)

            dve.wait_ge(w_hi, 1)
            split_lo(WH[:, 0, :, :], WH[:, 1, :, :], pZ).then_inc(prep_v, 1)
            for l in range(L):
                dve.wait_ge(w_hi, 2 + l)
                split_lo(WC[:, l, 0, :, :], WC[:, l, 1, :, :], MERGE[l % 3]).then_inc(wsplit_l, 1)
                if l == 1:
                    cast_adjacency(0, 0)
            dve.wait_ge(prep_t, 3 + L)
            link(v.tensor_copy(COLS[:, :], pIN[:, 0:COLS.shape[1]]))
            v.tensor_tensor(BRZ[:, :], BI[:, 0:2], BH[:, 0:2], ALU.add)
            v.tensor_scalar(BHN[:, :], BH[:, 2:3], WSCALE, None, ALU.mult).then_inc(cols_v, 1)
            aggregated_lo(0, 0)
            cast_adjacency(1, 1)
            cast_adjacency(2, 2)
            for q in range(Q):
                v.tensor_copy(I32[S * q:S * q + S, :], IDF[S * q:S * q + S, S * q:S * q + S])
            def iteration(k, s):
                if 0 <= s - 1 < K:
                    j, b = k - 1, graph_of(k - 1)
                    h_in = H[:, one(b), :]
                    h_out = H[:, one(b), :] if s - 1 < LAST else HF[:, (s - 1) % 2, :]
                    if s - 1 < LAST:
                        dve.wait_ge(n_a, j + 1)
                    if s < B - 1:
                        dve.wait_ge(hm, B if s == B - 2 else j + 1)
                    if s - 1 < LAST:
                        v.tensor_tensor(E[:, :], h_in, NN[:, :], ALU.subtract).then_inc(d_v, 1)
                if s + 1 < K:
                    aggregated_lo(k + 1, s + 1)
                if LAST <= s - 3 < K:
                    f = k - 3 - LAST
                    dve.wait_ge(f_y, f + 1)
                    for i in range(NI):
                        last = v.bn_stats(ST[:, i, :], Y[:, (s - 3) % 4, i, :])
                    last.then_inc(f_st, 1)
                if 0 <= s - 1 < K:
                    dve.wait_ge(d_v, j + 1)
                    dve.wait_ge(sig_z, j + 1)
                    v.tensor_tensor(E[:, :], E[:, :], Z[:, :], ALU.mult).then_inc(e_v, 1)
                if 0 <= s - 1 < K:
                    dve.wait_ge(e_v, j + 1)
                    if s - 1 >= LAST + 2:
                        dve.wait_ge(f_mm, j - LAST - 1)
                    v.tensor_tensor(h_out, E[:, :], NN[:, :], ALU.add).then_inc(h_v, 1)
                if s < K:
                    dve.wait_ge(sig_r, k + 1)
                    if s > 0:
                        dve.wait_ge(n_a, k)
                    v.scalar_tensor_tensor(out=T[:, :], in0=pHN[:, :], scalar=BHN[:, 0:1], in1=R[:, :],
                                           op0=ALU.add, op1=ALU.mult).then_inc(t_v, 1)
                if LAST <= s - 2 < K:
                    f = k - 2 - LAST
                    dve.wait_ge(f_mm, f + 1)
                    if s - 2 > LAST:
                        dve.wait_ge(f_y, f)
                    v.tensor_tensor(YM[:, :, :], pF[:, :].rearrange("p (i d) -> p i d", i=NI),
                                    MASK[:, one(f), :].rearrange("p b i -> p i b").to_broadcast([P, NI, D]), ALU.mult).then_inc(f_ym, 1)
                if s < K:
                    dve.wait_ge(t_v, k + 1)
                    dve.wait_ge(in_mm, k + 1)
                    v.tensor_tensor(T[:, :], pIN[:, :], T[:, :], ALU.add).then_inc(u_v, 1)
                if 0 <= s - 1 < LAST:
                    b = graph_of(k - 1)
                    dve.wait_ge(h_hi, k)
                    v.tensor_tensor(HT[:, one(b), 1, :], H[:, one(b), :], HT[:, one(b), 0, :],
                                    ALU.subtract).then_inc(h_lo, 1)
                if s + 3 < B:
                    cast_adjacency(k + 3, s + 3)
                if LAST <= s - 3 < K:
                    dve.wait_ge(f_st, k - 2 - LAST)
                if LAST <= s - 4 < K:
                    f, w, n = k - 4 - LAST, (s - 4) % 4, (s - 4) % 4
                    dve.wait_ge(f_rs, f + 1)
                    v.scalar_tensor_tensor(out=NB[:, w, :], in0=MV[:, w, :, 0], scalar=-1.0, in1=RS[:, w, 0:NI],
                                           op0=ALU.mult, op1=ALU.mult)
                    v.tensor_scalar(X1[S * n:S * n + S, one(quarter(f)), :], Y[0:S, n, 0:1, :],
                                    MV[0:S, w, 0, 0:1], RS[0:S, w, NI:NI + 1],
                                    ALU.subtract, ALU.mult).then_inc(f_nb, 1)
                if LAST <= s - 3 < K:
                    f, w = k - 3 - LAST, (s - 3) % 4
                    for i in range(NI):
                        last = v.bn_aggr(MV[:, w, i, :], ST[:, i, :])
                    last.then_inc(f_mv, 1)
                    dve.wait_ge(f_mv, f + 1)
                    v.tensor_scalar(VE[:, w, 0:NI], MV[:, w, :, 1], 1.0 + EPS, EPS * EPS, ALU.mult, ALU.add)
                    v.tensor_scalar(VE[:, w, NI:NI + 1], MV[:, w, 0:1, 1], EPS, None, ALU.add).then_inc(f_var, 1)

            def sum_degrees():
                dve.wait_ge(am_p, 1)
                link(v.tensor_reduce(DG[0], AMF, AX_X, ALU.add))
                link(v.tensor_scalar(DG[2], DG[0], 0.0, None, ALU.is_equal))
                v.tensor_tensor(DG[0], DG[0], DG[2], ALU.add)
                link(v.tensor_scalar(DG[1], DG[2], -1.0, 1.0, ALU.mult, ALU.add))
                v.tensor_copy(DG[2], DG[1]).then_inc(deg_v, 1)

            def transpose_adjacency():
                dve.wait_ge(am_p, 2)
                v.transpose(AT.rearrange("p g c m -> p (g c m)").bitcast(U32),
                            AM.rearrange("p g c m -> p (g c m)").bitcast(U32)).then_inc(deg_v, 1)
                link(v.transpose(CMT[:, :, :].bitcast(U32).rearrange("p g s -> p (g s)"),
                                 CM[:, :, :].bitcast(U32).rearrange("p g s -> p (g s)")))
                v.tensor_tensor(MS[:, :], FW[:, :], CMT[:, :, 0], ALU.mult)

            walk(dve, iteration, {63: sum_degrees, 64: transpose_adjacency})

            for t in range(G + 4):
                if 0 <= t < G:
                    dve.wait_ge(c_a, t + 1)
                    v.tensor_copy(YT[:, t, :], (pAG, pF)[t % 2][:, :]).then_inc(c_ae, 1)
                if 0 <= t - 3 < G:
                    g = t - 3
                    dve.wait_ge(c_d, g + 1)
                    u = U[:, g % 2, :, :]
                    v.tensor_tensor(u, pA2[:, g % 2, :].rearrange("p (c e) -> p c e", c=NC),
                                    B2S[:, g:g + 1, :].to_broadcast([P, NC, D]), ALU.add).then_inc(c_u, 1)
                    dve.wait_ge(c_u, g + 1)
                    v.tensor_scalar(u, u, 0.0, MS[:, g:g + 1], ALU.max, ALU.mult).then_inc(c_m, 1)
                    dve.wait_ge(c_m, g + 1)
                    if g > 0:
                        dve.wait_ge(c_f, g)
                    v.tensor_tensor(FU, X1[:, :, :] if g == 0 else FU, u, ALU.add).then_inc(c_f, 1)
            dve.wait_ge(c_f, G)
            for c in range(NC):
                last = v.bn_stats(ST[:, c, :], FU[:, c, :])
            last.then_inc(z_v, 1)
            dve.wait_ge(z_v, 1)
            for c in range(NC):
                last = v.bn_aggr(MV[:, 0, c, :], ST[:, c, :])
            last.then_inc(z_v, 1)
            dve.wait_ge(z_v, 2)
            v.tensor_scalar(VE[:, 0, 0:NC], MV[:, 0, :, 1], EPS, None, ALU.add).then_inc(z_v, 1)
            dve.wait_ge(z_p, 1)
            for c in range(NC):
                last = v.tensor_scalar(ZO[:, c, :], FU[:, c, :], MV[:, 0, c, 0:1], RS[:, 0, c:c + 1],
                                       ALU.subtract, ALU.mult)
            last.then_inc(z_o, 1)


_INS = ['x', 'adj', 'nodemask', 'L0_gnn_weight', 'L0_gnn_w_ih', 'L0_gnn_w_hh', 'L0_gnn_b_ih', 'L0_gnn_b_hh',
        'L1_gnn_W1', 'L1_gnn_b1', 'L1_gnn_W2', 'L1_gnn_b2', 'L1_gnn_fusion_w']


def kernel(**inputs):
    import numpy as _np
    import concourse.bacc as _bacc
    from concourse.bass_utils import run_bass_kernel_spmd as _run

    nc = _bacc.Bacc("TRN2", target_bir_lowering=False, num_devices=1)
    arrays, args = {}, []
    for name in _INS:
        a = _np.ascontiguousarray(inputs[name])
        arrays[f"in_{name}_dram"] = a
        args.append(nc.dram_tensor(f"in_{name}_dram", a.shape, mybir.dt.from_np(a.dtype), kind="ExternalInput").ap())
    args.append(nc.dram_tensor("out_dram", (B, N, D), F32, kind="ExternalOutput").ap())
    graph_net_kernel(nc, *args)
    r = _run(nc, [arrays], core_ids=[0])
    return r.results[0]["out_dram"]
```

```python
from contextlib import ExitStack

import concourse.bass as bass
from concourse import mybir

ALU = mybir.AluOpType
ACT = mybir.ActivationFunctionType
AX_X = mybir.AxisListType.X
F32 = mybir.dt.float32
F16 = mybir.dt.float16
U32 = mybir.dt.uint32

P = 128
B, N, D = 16, 512, 128
L = 5
NI = N // P
K = B * L
LAST = K - B
GROUPS = [list(range(25)), [0, 1, 2, 3, 4, 5, 6, 7, 8], [0, 9, 10, 11, 12, 13, 14],
          [6, 7, 8, 12, 13, 14], [3, 4, 5, 9, 10, 11]]
G = len(GROUPS)
HID = 256
NH = HID // P
Q = 4
S = P // Q
NC = B // Q
EPS = 1e-5
WARM_UP = 7
WSCALE = 1024.0
UNSCALE = 1.0 / WSCALE

MIDDLE = (14, 62)
SEGMENTS = [0, (1, 13), 13, MIDDLE, 62, 63, 64, 65, 66, 67, 68, 69, 70, (71, 79), 79]
assert (B, L) == (16, 5)
PARTS = [(0, 2), (2, 3), (3, 4)]
JOBS = G * len(PARTS)
PE_END = [("conv", 1), ("step", 80), ("conv", 2), ("step", 81)] + [("conv", t) for t in range(3, JOBS + 3)]
ACT_END = [("conv", 1), ("step", 80), ("conv", 2), ("conv", 3), ("conv", 4), ("conv", 5), ("block", 0), ("conv", 6),
           ("block", 1), ("conv", 7), ("block", 2), ("conv", 8), ("block", 3), ("conv", 9), ("block", 4),
           ("conv", 10), ("block", 5), ("conv", 11), ("block", 6), ("conv", 12), ("block", 7)] + [
    ("conv", t) for t in range(13, JOBS + 2)]
DVE_END = [("step", 80), ("step", 81), ("conv", 3), ("step", 82), ("conv", 4), ("step", 83)] + [
    ("conv", t) for t in range(5, 9)] + [("normalise", 78), ("stats", 0), ("conv", 9), ("out", 0),
    ("conv", 10), ("normalise", 79)] + [
    ("conv", t) for t in range(11, 14)] + [("stats", 1), ("conv", 14), ("out", 1)] + [
    ("conv", t) for t in range(15, JOBS + 4)] + [("stats", 2), ("out", 2)]


def walk(eng, iteration, before=None):
    for seg in SEGMENTS:
        if isinstance(seg, int):
            if before and seg in before:
                before[seg]()
            iteration(seg, seg)
        else:
            with eng.Fori(seg[0], seg[1] - 3, 4) as k0:
                for j in range(4):
                    iteration(k0 + j, seg[0] + j)


def finish(order, iteration, **parts):
    for what, n in order:
        if what == "step":
            iteration(n, n)
        else:
            parts[what](n)


def job_of(j):
    return (j % G, *PARTS[j // G])


def members_of(g, flat):
    rows = S if max(GROUPS[g]) >= S // 2 else S // 2
    return flat.rearrange("p (x n) -> p x n", n=S)[:, :, 0:rows]


def graph_of(k):
    return k % B if isinstance(k, int) else (k & (B - 1))


def layer_of(k):
    return k // B if isinstance(k, int) else (k >> 4)


def half(k):
    return k // 2 if isinstance(k, int) else (k >> 1)


def quarter(k):
    return k // 4 if isinstance(k, int) else (k >> 2)


def runs_of(members):
    runs = []
    for m in members:
        if runs and runs[-1][-1] == m - 1:
            runs[-1].append(m)
        else:
            runs.append([m])
    return runs


def one(i):
    return slice(i, i + 1) if isinstance(i, int) else bass.ds(i, 1)


def graph_net_kernel(nc, x, adj, nodemask, weight, w_ih, w_hh, b_ih, b_hh, W1, b1, W2, b2, fusion_w, out):
    ctx = ExitStack()
    with ctx:
        def sb(name, shape, dt):
            return ctx.enter_context(nc.sbuf_tensor(name, shape, dt))

        def pb(name, shape):
            return ctx.enter_context(nc.psum_tensor(name, shape, F32))

        def sem(name):
            return ctx.enter_context(nc.semaphore(name))

        A16 = sb("A16", [P, B, NI, N], F16)
        HT = sb("HT", [P, B, 2, N], F16)
        H = sb("H", [P, B, N], F32)
        AS = sb("AS", [P, 2, NI, N], F32)
        XS = sb("XS", [P, 4, NI, D], F32)
        NAT = sb("NAT", [P, 2, 2, NI, D], F16)
        AG = sb("AG", [P, 2, 2, N], F16)
        HF = sb("HF", [P, 2, N], F32)
        Y = sb("Y", [P, 4, NI, D], F32)
        R = sb("R", [P, N], F32)
        Z = sb("Z", [P, N], F32)
        T = sb("T", [P, N], F32)
        NN = sb("NN", [P, N], F32)
        E = sb("E", [P, N], F32)
        WC = sb("WC", [P, L, 2, 3, D], F16)
        WH = sb("WH", [P, 2, 3, D], F16)
        BRZ = sb("BRZ", [P, 2], F32)
        BHN = sb("BHN", [P, 1], F32)
        IDF = sb("IDF", [P, P], F32)
        I32 = sb("I32", [P, S], F32)
        rows_m, rows_i, rows_h, rows_1 = 0, B * NI, B * NI + 3, B * NI + 6
        ROWS = sb("ROWS", [rows_1 + G * NH, P], F32)
        COLS = sb("COLS", [P, rows_1 + G * NH], F32)
        MASK = COLS[:, 0:rows_i].rearrange("p (b i) -> p b i", b=B)
        BI = COLS[:, rows_i:rows_h]
        BH = COLS[:, rows_h:rows_1]
        B1 = COLS[:, rows_1:].rearrange("p (g j) -> p g j", g=G)
        ST = sb("ST", [P, NI, 6], F32)
        MV = sb("MV", [P, 4 + len(PARTS), NI, 2], F32)
        VE = sb("VE", [P, 4 + len(PARTS), NI + 1], F32)
        RS = sb("RS", [P, 4 + len(PARTS), NI + 1], F32)
        NB = sb("NB", [P, 4, NI], F32)
        NHALF = sb("NHALF", [P, G * NC], F32)
        BD = sb("BD", [P, G, NC, Q, S], F32)
        X1 = sb("X1", [P, NC, D], F32)
        CM = sb("CM", [P, G, S], F32)
        CMT = sb("CMT", [P, G, S], F32)
        FW = sb("FW", [P, G], F32)
        FS = sb("FS", [P, 4], F32)
        MS = sb("MS", [P, G], F32)
        DEG = sb("DEG", [P, 3, G * NC], F32)
        DG = [DEG[:, i, :] for i in range(3)]

        scr = A16[:, B - 4:B, :, :].rearrange("p b i n -> p (b i n)").bitcast(F32)
        off = [0]

        def scratch(n):
            off[0] += n
            assert off[0] <= 4 * NI * N // 2
            return scr[:, off[0] - n:off[0]]

        WL = scratch(L * D).rearrange("p (l e) -> p l e", l=L)
        WLT = scratch(L * D).rearrange("p (l e) -> p l e", l=L)
        WI = scratch(3 * D).rearrange("p (g e) -> p g e", g=3)
        WHS = scratch(3 * D).rearrange("p (g e) -> p g e", g=3)
        WIT = scratch(3 * D)
        y_flat = Y[:, :, :, :].rearrange("p s i d -> p (s i d)")
        y_end = G * NC * S
        AM = y_flat[:, 0:y_end].rearrange("p (g c m) -> p g c m", g=G, c=NC)
        AT = y_flat[:, y_end:2 * y_end].rearrange("p (g c m) -> p g c m", g=G, c=NC)
        AB = y_flat[:, 2 * y_end:2 * y_end + NC * S].rearrange("p (c m) -> p c m", c=NC)
        AMF = y_flat[:, 0:y_end].rearrange("p (x m) -> p x m", m=S)

        as_flat = AS[:, :, :, :].rearrange("p s i n -> p (s i n)")
        W1S = as_flat[:, 0:G * HID].rearrange("p (g e) -> p g e", g=G)
        W2S = as_flat[:, G * HID:2 * G * HID].rearrange("p (g j e) -> p g j e", g=G, j=NH)
        B2S = as_flat[:, 2 * G * HID:2 * G * HID + G * D].rearrange("p (g e) -> p g e", g=G)
        w_end = 2 * G * HID + G * D
        YM = as_flat[:, w_end:w_end + NI * D].rearrange("p (i d) -> p i d", i=NI)
        lateA = A16[:, :, :, :].rearrange("p b i n -> p (b i n)").bitcast(F32)
        YT = lateA[:, 0:G * N].rearrange("p (g n) -> p g n", g=G)
        H1 = lateA[:, G * N:3 * G * N].rearrange("p (g j n) -> p g j n", g=G, j=NH)
        S2 = lateA[:, 3 * G * N:4 * G * N].rearrange("p (g c e) -> p g c e", g=G, c=NC)
        U = lateA[:, 4 * G * N:(4 * G + 2) * N].rearrange("p (s c e) -> p s c e", s=2, c=NC)
        FU = lateA[:, (4 * G + 2) * N:(4 * G + 3) * N].rearrange("p (c e) -> p c e", c=NC)
        ZO = lateA[:, (4 * G + 3) * N:(4 * G + 4) * N].rearrange("p (c e) -> p c e", c=NC)

        pAG = pb("pAG", [P, N])
        pR = pb("pR", [P, N])
        pZ = pb("pZ", [P, N])
        pIN = pb("pIN", [P, N])
        pHN = pb("pHN", [P, N])
        pF = pb("pF", [P, N])
        pA2 = pb("pA2", [P, 2, N])

        MERGE = (pF, pAG, pR, pHN, pZ)

        ld_x = [sem(f"ld_x{i}") for i in range(4)]
        ld_a = [sem(f"ld_a{i}") for i in range(2)]
        ld_w = sem("ld_w")
        ld_l = sem("ld_l")
        ld_r = sem("ld_r")
        ld_c = sem("ld_c")
        ld_f = sem("ld_f")
        ld_g = sem("ld_g")
        st_y = [sem(f"st_y{i}") for i in range(4)]
        st_z = sem("st_z")
        ident = sem("ident")
        masks0 = sem("masks0")
        prep_t = sem("prep_t")
        prep_v = sem("prep_v")
        prep_a = sem("prep_a")
        wsplit_l = sem("wsplit_l")
        w_hi = sem("w_hi")
        cols_v = sem("cols_v")
        fw_max = sem("fw_max")
        chain = sem("chain")
        deg_v = sem("deg_v")
        BD_STEPS = 4 + Q
        bd_p = sem("bd_p")
        am_p = sem("am_p")
        nat_hi = sem("nat_hi")
        nat_lo = sem("nat_lo")
        a_cast = sem("a_cast")
        turn = [sem(f"turn{i}") for i in range(2)]
        hm = sem("hm")
        ag_mm = sem("ag_mm")
        ag_hi = sem("ag_hi")
        ag_lo = sem("ag_lo")
        r_mm = sem("r_mm")
        in_mm = sem("in_mm")
        z_mm = sem("z_mm")
        sig_r = sem("sig_r")
        sig_z = sem("sig_z")
        t_v = sem("t_v")
        u_v = sem("u_v")
        n_a = sem("n_a")
        d_v = sem("d_v")
        e_v = sem("e_v")
        h_v = sem("h_v")
        h_hi = sem("h_hi")
        h_lo = sem("h_lo")
        f_mm = sem("f_mm")
        f_ym = sem("f_ym")
        f_y = sem("f_y")
        f_st = sem("f_st")
        f_mv = sem("f_mv")
        f_var = sem("f_var")
        f_rs = sem("f_rs")
        f_nb = sem("f_nb")
        f_on = sem("f_on")
        f_dn = sem("f_dn")
        c_a = sem("c_a")
        c_ae = sem("c_ae")
        c_b = sem("c_b")
        c_be = sem("c_be")
        c_s = sem("c_s")
        c_se = sem("c_se")
        c_d = sem("c_d")
        c_u = sem("c_u")
        c_f = sem("c_f")
        z_v = sem("z_v")
        z_p = sem("z_p")
        z_o = sem("z_o")

        block = ctx.enter_context(nc.Block())

        @block.sync
        def _(sp):
            def load_x(slot, b):
                sp.dma_start(XS[:, slot, :, :],
                             x[one(b), :, :].rearrange("b (i p) d -> p (b i) d", p=P)).then_inc(ld_x[slot], 16)

            def load_a(slot, b):
                sp.dma_start(AS[:, slot, :, :],
                             adj[one(b), :, :].rearrange("b (i p) n -> p (b i) n", p=P)).then_inc(ld_a[slot], 16)

            sp.dma_start(WI, w_ih.rearrange("(g c) d -> c g d", c=P)).then_inc(ld_w, 16)
            sp.dma_start(WHS, w_hh.rearrange("(g c) d -> c g d", c=P)).then_inc(ld_w, 16)
            sp.dma_start(WL, weight.rearrange("l d e -> d l e")).then_inc(ld_l, 16)
            load_a(0, 0)
            load_a(1, 1)
            for row, src in ((rows_m, nodemask.rearrange("b (i p) -> (b i) p", p=P)),
                             (rows_i, b_ih.rearrange("(g p) -> g p", p=P)),
                             (rows_h, b_hh.rearrange("(g p) -> g p", p=P)),
                             (rows_1, b1.rearrange("g (j p) -> (g j) p", p=P))):
                sp.dma_start(ROWS[row:row + src.shape[0], :], src).then_inc(ld_r, 16)
            load_x(2, 2)
            load_x(3, 3)

            def transpose_x(b, s):
                sp.wait_ge(nat_lo, b + 1)
                sp.dma_start_transpose(HT[:, one(b), :, :].rearrange("p b h (i n) -> p (b h i) n", i=NI),
                                       NAT[:, s % 2, :, :, :].rearrange("p h i d -> p (h i d)"))\
                    .then_inc(turn[s % 2], 16)

            def transpose_h(k, s, b):
                sp.wait_ge(ag_mm, k - 1)
                sp.dma_start_transpose(NAT[:, s % 2, :, :, :].rearrange("p h i d -> p (h i) d"),
                                       HT[:, one(b), :, :].rearrange("p b h n -> p (b h n)"))\
                    .then_inc(turn[s % 2], 16)

            def next_a(k, s):
                sp.wait_ge(a_cast, k - 1)
                load_a(s % 2, k)

            def next_x(k, s):
                sp.wait_ge(nat_lo, k - 3)
                load_x(s % 4, k)

            def late_loads():
                for b in range(4):
                    sp.wait_ge(nat_lo, B - 3 + b)
                    load_x(b, b)
                for q in range(Q):
                    sp.dma_start(AB[S * q:S * q + S, :, :],
                                 adj.rearrange("(c q) n m -> q n c m", q=Q)[q, 0:S, :, 0:S]).then_inc(ld_c, 16)
                sp.wait_ge(a_cast, B)
                sp.dma_start(W1S, W1.rearrange("g d e -> d g e")).then_inc(ld_g, 16)
                sp.dma_start(W2S, W2.rearrange("g (j h) e -> h g j e", j=NH)).then_inc(ld_g, 16)
                sp.dma_start(B2S, b2.partition_broadcast(P)).then_inc(ld_g, 16)

            def store_y(b, slot):
                if isinstance(b, int) and b >= B - 2:
                    sp.wait_ge(f_dn, b - (B - 3))
                else:
                    sp.wait_ge(f_on, b + 1)
                sp.dma_start(out[one(b), S:P, :].rearrange("b p d -> p (b d)"),
                             Y[S:P, slot, 0, :]).then_inc(st_y[slot], 16)
                sp.dma_start(out[one(b), P:N, :].rearrange("b (i p) d -> p (b i) d", p=P),
                             Y[:, slot, 1:NI, :]).then_inc(st_y[slot], 16)

            def next_x_again(f, slot):
                sp.wait_ge(f_y, f + 1)
                load_x(slot, f + 4)

            transpose_x(0, 0)
            transpose_x(1, 1)
            for b in range(2, 4):
                next_a(b, b)
            next_x(4, 4)
            for b in range(2, 4):
                transpose_x(b, b)
                next_a(b + 2, b + 2)
                next_x(b + 3, b + 3)
            with sp.Fori(4, 9, 4) as b0:
                for j in range(4):
                    transpose_x(b0 + j, j)
                    next_a(b0 + j + 2, j + 2)
                    next_x(b0 + j + 3, j + 3)
            for b in range(12, B):
                transpose_x(b, b)
                if b + 2 < B:
                    next_a(b + 2, b + 2)
                if b + 3 < B:
                    next_x(b + 3, b + 3)
            for i in range(2):
                sp.wait_ge(turn[i], 16 * (B // 2))
            with sp.Fori(1, L - 1) as l:
                with sp.Fori(0, B - 3, 4) as b0:
                    for j in range(4):
                        transpose_h(l * B + b0 + j, j, b0 + j)
            late_loads()
            for b in range(8):
                transpose_h(LAST + b, b, b)
                if b >= 5:
                    next_x_again(b - 5, b - 5)
            with sp.Fori(8, B - 3, 4) as b0:
                for j in range(4):
                    transpose_h(b0 + LAST + j, j, b0 + j)
                    store_y(b0 - 8 + j, j)
                    next_x_again(b0 - 5 + j, (j + 3) % 4)
            next_x_again(B - 5, 3)
            for f in range(8, B):
                store_y(f, f % 4)
            for part, (c0, c1) in enumerate(PARTS):
                sp.wait_ge(z_o, part + 1)
                for c in range(c0, c1):
                    sp.dma_start(out[Q * c:Q * c + Q, 0:S, :], ZO[:, c, :]).then_inc(st_z, 16)
            for slot in range(4):
                sp.wait_ge(st_y[slot], 32 * (B // 4))
            sp.wait_ge(st_z, 16 * NC)

        @block.gpsimd
        def _(pool):
            nc.gpsimd.memset(IDF[:, :], 0.0).then_inc(ident, 1)
            pool.wait_ge(ident, 1)
            nc.gpsimd.affine_select(out=IDF[:, :], in_=IDF[:, :], compare_op=ALU.not_equal, fill=1.0,
                                    base=0, pattern=[[-1, P]], channel_multiplier=1).then_inc(ident, 1)
            nc.gpsimd.memset(NHALF[:, :], -0.5)
            nc.gpsimd.memset(CM[:, :, :], 0.0).then_inc(masks0, 1)
            pool.wait_ge(masks0, 1)
            for g, members in enumerate(GROUPS):
                for run in runs_of(members):
                    last = nc.gpsimd.memset(CM[:, g, run[0]:run[-1] + 1], 1.0)
            last.then_inc(masks0, 1)

            def natural_lo(k, s):
                pool.wait_ge(nat_hi, k + 1)
                nc.gpsimd.tensor_tensor(NAT[:, s % 2, 1, :, :], XS[:, s % 4, :, :], NAT[:, s % 2, 0, :, :],
                                        ALU.subtract).then_inc(nat_lo, 1)

            def iteration(k, s):
                if LAST <= s - 1 < K - 1:
                    pool.wait_ge(n_a, k)
                    pool.wait_ge(h_v, k - 1)
                    nc.gpsimd.tensor_tensor(E[:, :], H[:, one(graph_of(k - 1)), :], NN[:, :],
                                            ALU.subtract).then_inc(d_v, 1)
                if s + 3 < B:
                    natural_lo(k + 3, s + 3)
                if s + 2 < B:
                    b = graph_of(k + 2)
                    pool.wait_ge(turn[s % 2], 16 * (half(k + 2) + 1))
                    nc.gpsimd.tensor_tensor(H[:, one(b), :], HT[:, one(b), 0, :], HT[:, one(b), 1, :],
                                            ALU.add).then_inc(hm, 1)
                if LAST <= s - 3 < K - 1:
                    f, slot = k - 3 - LAST, (s - 3) % 4
                    pool.wait_ge(f_ym, f + 1)
                    if s - 3 >= LAST + 4:
                        pool.wait_ge(st_y[slot], 32 * quarter(f))
                    pool.wait_ge(ld_x[slot], 16 * (B // 4) + 16 * (quarter(f) + 1))
                    nc.gpsimd.tensor_tensor(Y[:, slot, :, :], YM[:, :, :], XS[:, slot, :, :],
                                            ALU.add).then_inc(f_y, 1)
                if LAST <= s - 4 < K:
                    f, w = k - 4 - LAST, (s - 4) % 4
                    pool.wait_ge(f_var, f + 1)
                    nc.gpsimd.tensor_tensor(RS[:, w, :], VE[:, w, :], NHALF[:, 0:NI + 1], ALU.pow).then_inc(f_rs, 1)

            natural_lo(0, 0)
            natural_lo(1, 1)
            natural_lo(2, 2)
            for b in range(2):
                pool.wait_ge(turn[b], 16)
                nc.gpsimd.tensor_tensor(H[:, b, :], HT[:, b, 0, :], HT[:, b, 1, :], ALU.add).then_inc(hm, 1)

            def prepare_adjacency():
                g_ = nc.gpsimd
                n = [0]

                def link(ins):
                    n[0] += 1
                    ins.then_inc(bd_p, 1)
                    pool.wait_ge(bd_p, n[0])

                pool.wait_ge(ld_c, 16 * Q)
                for g in range(G):
                    last = g_.tensor_tensor(AM[:, g, :, :], AB[:, :, :],
                                            CM[:, g:g + 1, :].to_broadcast([P, NC, S]), ALU.mult)
                link(last)
                link(g_.tensor_tensor(AMF, AMF, I32[:, None, :].to_broadcast([P, G * NC, S]), ALU.add))
                g_.memset(BD[:, :, :, :, :].rearrange("p g c q s -> p (g c q s)"), 0.0).then_inc(am_p, 1)
                pool.wait_ge(deg_v, 1)
                link(g_.tensor_tensor(DG[1], DG[0], NHALF[:, :], ALU.pow))
                link(g_.tensor_tensor(DG[2], DG[2], DG[1], ALU.mult))
                g_.tensor_tensor(AMF, AMF, DG[2][:, :, None].to_broadcast([P, G * NC, S]), ALU.mult).then_inc(am_p, 1)
                pool.wait_ge(deg_v, 2)
                pool.wait_ge(am_p, 2)
                for q in range(Q):
                    rows = slice(S * q, S * q + S)
                    link(g_.tensor_tensor(BD[rows, :, :, q, :].rearrange("p g c s -> p (g c) s"),
                                            AT[rows, :, :, :].rearrange("p g c m -> p (g c) m"),
                                            DG[2][rows, :, None].to_broadcast([S, G * NC, S]), ALU.mult))

                assert n[0] == BD_STEPS

            walk(pool, iteration, {62: prepare_adjacency})
            for k in range(K, K + 4):
                iteration(k, k)
            for part, (c0, c1) in enumerate(PARTS):
                pool.wait_ge(z_v, 3 * part + 3)
                nc.gpsimd.tensor_tensor(RS[:, 4 + part, c0:c1], VE[:, 4 + part, c0:c1], NHALF[:, c0:c1],
                                        ALU.pow).then_inc(z_p, 1)

        @block.tensor
        def _(pe):
            mm = nc.tensor.matmul
            pe.wait_ge(ident, 2)
            for _ in range(WARM_UP):
                mm(pAG[:, 0:P], IDF[:, :], IDF[:, :], start=True, stop=True)
            pe.wait_ge(ld_w, 16 * 2)
            for g in range(3):
                nc.tensor.transpose(pR[:, g * D:(g + 1) * D], WI[:, g, :], IDF[:, :])
            last = None
            for g in range(3):
                last = nc.tensor.transpose(pZ[:, g * D:(g + 1) * D], WHS[:, g, :], IDF[:, :])
            last.then_inc(prep_t, 1)
            pe.wait_ge(ld_l, 16)
            for l in range(4):
                nc.tensor.transpose(pIN[:, l * D:(l + 1) * D], WL[:, l, :], IDF[:, :])
            nc.tensor.transpose(pHN[:, 0:D], WL[:, 4, :], IDF[:, :]).then_inc(prep_t, 1)

            def aggregate(k, s):
                b = graph_of(k)
                if s < B - 1:
                    pe.wait_ge(nat_lo, k + 1)
                    pe.wait_ge(a_cast, k + 1)
                else:
                    if s == B - 1:
                        pe.wait_ge(nat_lo, B)
                        pe.wait_ge(a_cast, B)
                    pe.wait_ge(turn[s % 2], 16 * (half(k) + 1))
                if s > 1:
                    pe.wait_ge(ag_lo, k - 1)
                for h in range(2):
                    for i in range(NI):
                        last = mm(pA2[:, s % 2, :], NAT[:, s % 2, h, i, :], A16[:, one(b), i, :],
                                  start=(h == 0 and i == 0), stop=(h == 1 and i == NI - 1))
                last.then_inc(ag_mm, 1)

            def split_product(bank, w_hi, w_lo, v_hi, v_lo, start, stop):
                mm(bank[:, :], w_hi, v_hi, start=start, stop=False)
                mm(bank[:, :], w_hi, v_lo, start=False, stop=False)
                return mm(bank[:, :], w_lo, v_hi, start=False, stop=stop)

            def gates(k, s, between):
                b = graph_of(k)
                l = layer_of(k) if MIDDLE[0] <= s < MIDDLE[1] else s // B
                ht = [HT[:, one(b), h, :] for h in range(2)]
                pe.wait_ge(turn[s % 2], 16 * (half(k) + 1))
                if s == 0:
                    pe.wait_ge(cols_v, 1)
                if s > 0:
                    pe.wait_ge(t_v, k)
                split_product(pHN, WH[:, 0, 2, :], WH[:, 1, 2, :], ht[0], ht[1], True, True)
                if s > 0:
                    pe.wait_ge(sig_r, k)
                split_product(pR, WH[:, 0, 0, :], WH[:, 1, 0, :], ht[0], ht[1], True, False)
                if s > 0:
                    pe.wait_ge(sig_z, k)
                split_product(pZ, WH[:, 0, 1, :], WH[:, 1, 1, :], ht[0], ht[1], True, False)
                between()
                ag = [AG[:, s % 2, h, :] for h in range(2)]

                def wc(h, g):
                    if isinstance(l, int):
                        return WC[:, l, h, g, :]
                    return WC[:, one(l), h, g, :].rearrange("p l d -> p (l d)")

                pe.wait_ge(ag_lo, k + 1)
                split_product(pR, wc(0, 0), wc(1, 0), ag[0], ag[1], False, True).then_inc(r_mm, 1)
                if s > 0:
                    pe.wait_ge(u_v, k)
                split_product(pIN, wc(0, 2), wc(1, 2), ag[0], ag[1], True, True).then_inc(in_mm, 1)
                split_product(pZ, wc(0, 1), wc(1, 1), ag[0], ag[1], False, True).then_inc(z_mm, 1)

            def back(k, s):
                pe.wait_ge(h_v, k + 1)
                if s > LAST:
                    pe.wait_ge(f_ym, k - LAST)
                for i in range(NI):
                    last = nc.tensor.transpose(pF[:, i * P:(i + 1) * P], HF[:, s % 2, i * P:(i + 1) * P], IDF[:, :])
                last.then_inc(f_mm, 1)

            def iteration(k, s):
                if s + 1 < K:
                    aggregate(k + 1, s + 1)
                if s < K:
                    gates(k, s, lambda: back(k - 2, s - 2) if s - 2 >= LAST else None)
                elif s - 2 < K:
                    back(k - 2, s - 2)

            pe.wait_ge(prep_v, 1)
            for l in range(L):
                if l == 3:
                    pe.wait_ge(prep_v, 2)
                mm(MERGE[l][:, 0:3 * D], WLT[:, l, :], WIT, start=True, stop=True).then_inc(prep_t, 1)
            aggregate(0, 0)
            pe.wait_ge(ld_r, 16 * 4)
            rows = ROWS.shape[0]
            nc.tensor.transpose(pIN[:, 0:rows], ROWS[:, :], IDF[0:rows, 0:rows]).then_inc(prep_t, 1)

            banks_s, banks_d = (pHN, pIN), (pA2[:, 0, :], pA2[:, 1, :])

            def conv_a(j):
                g, c0, c1 = job_of(j)
                if j == 0:
                    pe.wait_ge(ld_g, 48)
                    pe.wait_ge(bd_p, BD_STEPS)
                if g == 0:
                    pe.wait_ge(f_nb, Q * c1)
                if j >= 1:
                    pe.wait_ge(c_ae, j)
                for c in range(c0, c1):
                    last = mm(members_of(g, pAG[:, c * P:(c + 1) * P]), X1[:, c, :],
                              members_of(g, BD[:, g, c, :, :].rearrange("p q n -> p (q n)")),
                              start=True, stop=True)
                last.then_inc(c_a, 1)

            def conv_b(j):
                g, c0, c1 = job_of(j)
                pe.wait_ge(c_ae, j + 1)
                for h, bank in enumerate((pR, pZ)):
                    if j == 0:
                        pe.wait_ge((sig_r, sig_z)[h], K)
                    if j >= 1:
                        pe.wait_ge(c_be, NH * (j - 1) + h + 1)
                    mm(members_of(g, bank[:, c0 * P:c1 * P]), W1S[:, g, h * P:(h + 1) * P],
                       members_of(g, YT[:, g, c0 * P:c1 * P]), start=True, stop=True).then_inc(c_b, 1)

            def conv_s(j):
                g, c0, c1 = job_of(j)
                pe.wait_ge(c_be, NH * (j + 1))
                if j == 0:
                    pe.wait_ge(u_v, K)
                if j >= 2:
                    pe.wait_ge(c_se, j - 1)
                bank = banks_s[j % 2]
                for c in range(c0, c1):
                    for h in range(NH):
                        last = mm(bank[:, c * P:(c + 1) * P], H1[:, g, h, c * P:(c + 1) * P], W2S[:, g, h, :],
                                  start=(h == 0), stop=(h == NH - 1))
                last.then_inc(c_s, 1)

            def conv_d(j):
                g, c0, c1 = job_of(j)
                pe.wait_ge(c_se, j + 1)
                if j >= 2:
                    pe.wait_ge(c_u, j - 1)
                bank = banks_d[j % 2]
                for c in range(c0, c1):
                    last = mm(bank[:, c * P:(c + 1) * P], BD[:, g, c, :, :].rearrange("p q n -> p (q n)"),
                              S2[:, g, c, :], start=True, stop=True)
                last.then_inc(c_d, 1)

            def conv_turn(t):
                for fn, lag in ((conv_b, 1), (conv_a, 0), (conv_s, 2), (conv_d, 3)):
                    if 0 <= t - lag < JOBS:
                        fn(t - lag)

            walk(pe, iteration, {K - 1: lambda: conv_turn(0)})
            finish(PE_END, iteration, conv=conv_turn)

        @block.scalar
        def _(act):
            def natural_hi(k, s):
                act.wait_ge(ld_x[s % 4], 16 * (quarter(k) + 1))
                if s >= 2:
                    act.wait_ge(ag_mm, k - 1)
                    act.wait_ge(turn[s % 2], 16 * half(k))
                nc.scalar.activation(NAT[:, s % 2, 0, :, :], XS[:, s % 4, :, :], ACT.Copy).then_inc(nat_hi, 1)

            def aggregated_hi(k, s):
                act.wait_ge(ag_mm, k + 1)
                if s >= 2:
                    act.wait_ge(z_mm, k - 1)
                nc.scalar.activation(AG[:, s % 2, 0, :], pA2[:, s % 2, :], ACT.Copy).then_inc(ag_hi, 1)

            def state_hi(k, s):
                act.wait_ge(h_v, k + 1)
                b = graph_of(k)
                nc.scalar.activation(HT[:, one(b), 0, :], H[:, one(b), :], ACT.Copy).then_inc(h_hi, 1)

            def normalise(k, s, blocks=range(NI)):
                if 0 in blocks:
                    act.wait_ge(f_nb, k - LAST + 1)
                w = s % 4
                for i in blocks:
                    last = nc.scalar.activation(Y[:, w, i, :], Y[:, w, i, :], ACT.Identity,
                                                bias=NB[:, w, i:i + 1], scale=RS[:, w, i:i + 1])
                if NI - 1 in blocks:
                    last.then_inc(f_on, 1)

            def iteration(k, s):
                if s + 1 < K:
                    aggregated_hi(k + 1, s + 1)
                if s + 3 < B:
                    natural_hi(k + 3, s + 3)
                if LAST <= s - 5 < K:
                    normalise(k - 5, s - 5)
                if s < K:
                    act.wait_ge(r_mm, k + 1)
                    if s > 0:
                        act.wait_ge(t_v, k)
                    nc.scalar.activation(R[:, :], pR[:, :], ACT.Sigmoid, bias=BRZ[:, 0:1], scale=UNSCALE)\
                        .then_inc(sig_r, 1)
                if s < K:
                    if 0 <= s - 1 < LAST:
                        state_hi(k - 1, s - 1)
                    act.wait_ge(z_mm, k + 1)
                    if s > 0:
                        act.wait_ge(e_v, k)
                    nc.scalar.activation(Z[:, :], pZ[:, :], ACT.Sigmoid, bias=BRZ[:, 1:2], scale=UNSCALE)\
                        .then_inc(sig_z, 1)
                    act.wait_ge(u_v, k + 1)
                    if s > 0:
                        act.wait_ge(h_v, k)
                    nc.scalar.activation(NN[:, :], T[:, :], ACT.Tanh, bias=BI[:, 2:3], scale=UNSCALE)\
                        .then_inc(n_a, 1)

            act.dma_start(FW[:, :], fusion_w.partition_broadcast(P)).then_inc(ld_f, 16)
            for b in range(2):
                act.dma_start(XS[:, b, :, :], x[b, :, :].rearrange("(i p) d -> p i d", p=P)).then_inc(ld_x[b], 16)
            act.wait_ge(fw_max, 1)
            nc.scalar.activation(FW[:, :], FW[:, :], ACT.Exp, bias=FS[:, 0:1], scale=1.0).then_inc(prep_a, 1)
            natural_hi(0, 0)
            natural_hi(1, 1)
            act.wait_ge(prep_t, 1)
            nc.scalar.activation(WH[:, 0, :, :].rearrange("p g d -> p (g d)"), pZ[:, 0:3 * D], ACT.Copy,
                                 scale=WSCALE).then_inc(w_hi, 1)
            for l in range(L):
                act.wait_ge(prep_t, 3 + l)
                nc.scalar.activation(WC[:, l, 0, :, :].rearrange("p g d -> p (g d)"), MERGE[l][:, 0:3 * D],
                                     ACT.Copy, scale=WSCALE).then_inc(w_hi, 1)
            aggregated_hi(0, 0)
            natural_hi(2, 2)
            act.wait_ge(cols_v, 1)

            def conv_turn(t):
                if 0 <= t - 1 < JOBS:
                    j = t - 1
                    g, c0, c1 = job_of(j)
                    for h, bank in enumerate((pR, pZ)):
                        act.wait_ge(c_b, NH * j + h + 1)
                        nc.scalar.activation(members_of(g, H1[:, g, h, c0 * P:c1 * P]),
                                             members_of(g, bank[:, c0 * P:c1 * P]), ACT.Relu,
                                             bias=B1[:, g, h:h + 1]).then_inc(c_be, 1)
                if 0 <= t < JOBS:
                    g, c0, c1 = job_of(t)
                    act.wait_ge(c_a, t + 1)
                    nc.scalar.activation(members_of(g, YT[:, g, c0 * P:c1 * P]),
                                         members_of(g, pAG[:, c0 * P:c1 * P]), ACT.Copy).then_inc(c_ae, 1)
                if 0 <= t - 2 < JOBS:
                    j = t - 2
                    g, c0, c1 = job_of(j)
                    act.wait_ge(c_s, j + 1)
                    nc.scalar.activation(S2[:, g, c0:c1, :].rearrange("p c e -> p (c e)"),
                                         (pHN, pIN)[j % 2][:, c0 * P:c1 * P], ACT.Copy).then_inc(c_se, 1)

            def block_of(n):
                k = K - 4 + n // NI
                normalise(k, k, [n % NI])

            walk(act, iteration, {K - 1: lambda: conv_turn(0)})
            finish(ACT_END, iteration, conv=conv_turn, block=block_of)

        @block.vector
        def _(dve):
            v = nc.vector
            links = [0]

            def link(ins):
                links[0] += 1
                ins.then_inc(chain, 1)
                dve.wait_ge(chain, links[0])

            def cast_adjacency(k, s):
                dve.wait_ge(ld_a[s % 2], 16 * (half(k) + 1))
                v.tensor_scalar(A16[:, one(graph_of(k)), :, :].rearrange("p b i n -> p (b i n)"),
                                AS[:, s % 2, :, :].rearrange("p i n -> p (i n)"), 0.0, None,
                                ALU.not_equal).then_inc(a_cast, 1)

            def aggregated_lo(k, s):
                dve.wait_ge(ag_hi, k + 1)
                v.tensor_tensor(AG[:, s % 2, 1, :], pA2[:, s % 2, :], AG[:, s % 2, 0, :],
                                ALU.subtract).then_inc(ag_lo, 1)

            dve.wait_ge(ld_f, 16)
            link(v.tensor_reduce(FS[:, 1:2], FW[:, :], AX_X, ALU.max))
            v.tensor_scalar(FS[:, 0:1], FS[:, 1:2], -1.0, None, ALU.mult).then_inc(fw_max, 1)
            dve.wait_ge(prep_a, 1)
            link(v.tensor_reduce(FS[:, 2:3], FW[:, :], AX_X, ALU.add))
            link(v.reciprocal(FS[:, 3:4], FS[:, 2:3]))
            link(v.tensor_scalar(FW[:, :], FW[:, :], FS[:, 3:4], None, ALU.mult))
            dve.wait_ge(prep_t, 1)
            v.tensor_copy(WIT, pR[:, 0:3 * D])
            dve.wait_ge(prep_t, 2)
            v.tensor_copy(WLT[:, 0:4, :].rearrange("p l d -> p (l d)"), pIN[:, :]).then_inc(prep_v, 1)
            v.tensor_copy(WLT[:, 4, :], pHN[:, 0:D])

            def split_lo(dst_hi, dst_lo, bank):
                src = bank[:, 0:3 * D].rearrange("p (g d) -> p g d", g=3)
                return v.scalar_tensor_tensor(out=dst_lo, in0=src, scalar=WSCALE, in1=dst_hi,
                                              op0=ALU.mult, op1=ALU.subtract)

            dve.wait_ge(w_hi, 1)
            split_lo(WH[:, 0, :, :], WH[:, 1, :, :], pZ).then_inc(prep_v, 1)
            for l in range(L):
                dve.wait_ge(w_hi, 2 + l)
                split_lo(WC[:, l, 0, :, :], WC[:, l, 1, :, :], MERGE[l]).then_inc(wsplit_l, 1)
                if l == 0:
                    cast_adjacency(0, 0)
                if l == 2:
                    cast_adjacency(1, 1)
            dve.wait_ge(prep_t, 3 + L)
            link(v.tensor_copy(COLS[:, :], pIN[:, 0:COLS.shape[1]]))
            v.tensor_tensor(BRZ[:, :], BI[:, 0:2], BH[:, 0:2], ALU.add)
            v.tensor_scalar(BHN[:, :], BH[:, 2:3], WSCALE, None, ALU.mult).then_inc(cols_v, 1)
            aggregated_lo(0, 0)
            cast_adjacency(2, 2)
            for q in range(Q):
                v.tensor_copy(I32[S * q:S * q + S, :], IDF[S * q:S * q + S, S * q:S * q + S])

            def residual_stats(k, s):
                if LAST <= s - 3 < K:
                    f = k - 3 - LAST
                    dve.wait_ge(f_y, f + 1)
                    for i in range(NI):
                        last = v.bn_stats(ST[:, i, :], Y[:, (s - 3) % 4, i, :])
                    last.then_inc(f_st, 1)

            def layer_norm_scale(k, s):
                if LAST <= s - 4 < K:
                    f, w, n = k - 4 - LAST, (s - 4) % 4, (s - 4) % 4
                    dve.wait_ge(f_rs, f + 1)
                    v.scalar_tensor_tensor(out=NB[:, w, :], in0=MV[:, w, :, 0], scalar=-1.0, in1=RS[:, w, 0:NI],
                                           op0=ALU.mult, op1=ALU.mult)
                    v.tensor_scalar(X1[S * n:S * n + S, one(quarter(f)), :], Y[0:S, n, 0:1, :],
                                    MV[0:S, w, 0, 0:1], RS[0:S, w, NI:NI + 1],
                                    ALU.subtract, ALU.mult).then_inc(f_nb, 1)

            def iteration(k, s):
                if 0 <= s - 1 < K:
                    j, b = k - 1, graph_of(k - 1)
                    h_in = H[:, one(b), :]
                    h_out = H[:, one(b), :] if s - 1 < LAST else HF[:, (s - 1) % 2, :]
                    if s - 1 < LAST or s - 1 == K - 1:
                        dve.wait_ge(n_a, j + 1)
                    if s < B - 1:
                        dve.wait_ge(hm, B if s == B - 2 else j + 1)
                    if s - 1 < LAST or s - 1 == K - 1:
                        v.tensor_tensor(E[:, :], h_in, NN[:, :], ALU.subtract).then_inc(d_v, 1)
                if s + 1 < K:
                    aggregated_lo(k + 1, s + 1)
                if 0 <= s - 1 < K:
                    dve.wait_ge(d_v, j + 1)
                    dve.wait_ge(sig_z, j + 1)
                    v.tensor_tensor(E[:, :], E[:, :], Z[:, :], ALU.mult).then_inc(e_v, 1)
                if 0 <= s - 1 < K:
                    dve.wait_ge(e_v, j + 1)
                    if s - 1 >= LAST + 2:
                        dve.wait_ge(f_mm, j - LAST - 1)
                    v.tensor_tensor(h_out, E[:, :], NN[:, :], ALU.add).then_inc(h_v, 1)
                if s < K:
                    residual_stats(k, s)
                if s < K:
                    dve.wait_ge(sig_r, k + 1)
                    if s > 0:
                        dve.wait_ge(n_a, k)
                    v.scalar_tensor_tensor(out=T[:, :], in0=pHN[:, :], scalar=BHN[:, 0:1], in1=R[:, :],
                                           op0=ALU.add, op1=ALU.mult).then_inc(t_v, 1)
                if s < K:
                    dve.wait_ge(t_v, k + 1)
                    dve.wait_ge(in_mm, k + 1)
                    v.tensor_tensor(T[:, :], pIN[:, :], T[:, :], ALU.add).then_inc(u_v, 1)
                if 0 <= s - 1 < LAST:
                    b = graph_of(k - 1)
                    dve.wait_ge(h_hi, k)
                    v.tensor_tensor(HT[:, one(b), 1, :], H[:, one(b), :], HT[:, one(b), 0, :],
                                    ALU.subtract).then_inc(h_lo, 1)
                if LAST <= s - 2 < K:
                    f = k - 2 - LAST
                    dve.wait_ge(f_mm, f + 1)
                    if s - 2 > LAST:
                        dve.wait_ge(f_y, f)
                    v.tensor_tensor(YM[:, :, :], pF[:, :].rearrange("p (i d) -> p i d", i=NI),
                                    MASK[:, one(f), :].rearrange("p b i -> p i b").to_broadcast([P, NI, D]),
                                    ALU.mult).then_inc(f_ym, 1)
                if s - 2 == K - 1:
                    slot = (s - 2) % 4
                    dve.wait_ge(f_ym, B)
                    dve.wait_ge(f_y, B - 1)
                    dve.wait_ge(ld_x[slot], 16 * (B // 2))
                    dve.wait_ge(st_y[slot], 32 * (B // 4 - 1))
                    v.tensor_tensor(Y[:, slot, :, :], YM[:, :, :], XS[:, slot, :, :], ALU.add).then_inc(f_y, 1)
                if s >= K:
                    residual_stats(k, s)
                if s + 3 < B:
                    cast_adjacency(k + 3, s + 3)
                if LAST <= s - 3 < K:
                    dve.wait_ge(f_st, k - 2 - LAST)
                if s < K:
                    layer_norm_scale(k, s)
                if LAST <= s - 3 < K:
                    f, w = k - 3 - LAST, (s - 3) % 4
                    for i in range(NI):
                        last = v.bn_aggr(MV[:, w, i, :], ST[:, i, :])
                    last.then_inc(f_mv, 1)
                    dve.wait_ge(f_mv, f + 1)
                    v.tensor_scalar(VE[:, w, 0:NI], MV[:, w, :, 1], 1.0 + EPS, EPS * EPS, ALU.mult, ALU.add)
                    v.tensor_scalar(VE[:, w, NI:NI + 1], MV[:, w, 0:1, 1], EPS, None, ALU.add).then_inc(f_var, 1)
                if s >= K:
                    layer_norm_scale(k, s)

            def sum_degrees():
                dve.wait_ge(am_p, 1)
                link(v.tensor_reduce(DG[0], AMF, AX_X, ALU.add))
                link(v.tensor_scalar(DG[2], DG[0], 0.0, None, ALU.is_equal))
                v.tensor_tensor(DG[0], DG[0], DG[2], ALU.add)
                link(v.tensor_scalar(DG[1], DG[2], -1.0, 1.0, ALU.mult, ALU.add))
                v.tensor_copy(DG[2], DG[1]).then_inc(deg_v, 1)

            def transpose_adjacency():
                dve.wait_ge(am_p, 2)
                v.transpose(AT.rearrange("p g c m -> p (g c m)").bitcast(U32),
                            AM.rearrange("p g c m -> p (g c m)").bitcast(U32)).then_inc(deg_v, 1)
                link(v.transpose(CMT[:, :, :].bitcast(U32).rearrange("p g s -> p (g s)"),
                                 CM[:, :, :].bitcast(U32).rearrange("p g s -> p (g s)")))
                link(v.tensor_tensor(MS[:, :], FW[:, :], CMT[:, :, 0], ALU.mult))

            def scale_biases():
                dve.wait_ge(ld_g, 48)
                for g in range(G):
                    last = v.tensor_scalar(B2S[:, g, :], B2S[:, g, :], MS[:, g:g + 1], None, ALU.mult)
                link(last)

            def conv_turn(t):
                if 0 <= t - 3 < JOBS:
                    j = t - 3
                    g, c0, c1 = job_of(j)
                    dve.wait_ge(c_d, j + 1)
                    if j >= 2:
                        dve.wait_ge(c_f, j - 1)
                    v.scalar_tensor_tensor(out=U[:, j % 2, c0:c1, :],
                                           in0=pA2[:, j % 2, c0 * P:c1 * P].rearrange("p (c e) -> p c e", e=D),
                                           scalar=MS[:, g:g + 1],
                                           in1=B2S[:, g:g + 1, :].to_broadcast([P, c1 - c0, D]),
                                           op0=ALU.mult, op1=ALU.add).then_inc(c_u, 1)
                if 0 <= t - 4 < JOBS:
                    j = t - 4
                    g, c0, c1 = job_of(j)
                    fused = FU[:, c0:c1, :]
                    dve.wait_ge(c_u, j + 1)
                    if j > 0:
                        dve.wait_ge(c_f, j)
                    v.scalar_tensor_tensor(out=fused, in0=U[:, j % 2, c0:c1, :], scalar=0.0,
                                           in1=X1[:, c0:c1, :] if g == 0 else fused,
                                           op0=ALU.max, op1=ALU.add).then_inc(c_f, 1)

            def normalise(k):
                w = k % 4
                for i in range(NI):
                    last = v.tensor_scalar(Y[:, w, i, :], Y[:, w, i, :], MV[:, w, i, 0:1], RS[:, w, i:i + 1],
                                           ALU.subtract, ALU.mult)
                last.then_inc(f_dn, 1)

            def stats_of(part):
                c0, c1 = PARTS[part]
                dve.wait_ge(c_f, G * (part + 1))
                for c in range(c0, c1):
                    last = v.bn_stats(ST[:, c, :], FU[:, c, :])
                last.then_inc(z_v, 1)
                dve.wait_ge(z_v, 3 * part + 1)
                for c in range(c0, c1):
                    last = v.bn_aggr(MV[:, 4 + part, c, :], ST[:, c, :])
                last.then_inc(z_v, 1)
                dve.wait_ge(z_v, 3 * part + 2)
                v.tensor_scalar(VE[:, 4 + part, c0:c1], MV[:, 4 + part, c0:c1, 1], EPS, None, ALU.add).then_inc(z_v, 1)

            def out_of(part):
                c0, c1 = PARTS[part]
                dve.wait_ge(z_p, part + 1)
                for c in range(c0, c1):
                    last = v.tensor_scalar(ZO[:, c, :], FU[:, c, :], MV[:, 4 + part, c, 0:1], RS[:, 4 + part, c:c + 1],
                                           ALU.subtract, ALU.mult)
                last.then_inc(z_o, 1)

            walk(dve, iteration, {63: sum_degrees, 64: transpose_adjacency, 65: scale_biases})
            finish(DVE_END, iteration, conv=conv_turn, normalise=normalise, stats=stats_of,
                   out=out_of)


_INS = ['x', 'adj', 'nodemask', 'L0_gnn_weight', 'L0_gnn_w_ih', 'L0_gnn_w_hh', 'L0_gnn_b_ih', 'L0_gnn_b_hh',
        'L1_gnn_W1', 'L1_gnn_b1', 'L1_gnn_W2', 'L1_gnn_b2', 'L1_gnn_fusion_w']


def kernel(**inputs):
    import numpy as _np
    import concourse.bacc as _bacc
    from concourse.bass_utils import run_bass_kernel_spmd as _run

    nc = _bacc.Bacc("TRN2", target_bir_lowering=False, num_devices=1)
    arrays, args = {}, []
    for name in _INS:
        a = _np.ascontiguousarray(inputs[name])
        arrays[f"in_{name}_dram"] = a
        args.append(nc.dram_tensor(f"in_{name}_dram", a.shape, mybir.dt.from_np(a.dtype), kind="ExternalInput").ap())
    args.append(nc.dram_tensor("out_dram", (B, N, D), F32, kind="ExternalOutput").ap())
    graph_net_kernel(nc, *args)
    r = _run(nc, [arrays], core_ids=[0])
    return r.results[0]["out_dram"]
```
